# Optimizing a Trainium2 kernel written in Bass

```python
import numpy as np
import jax
import jax.numpy as jnp

def _softmax(x, axis=-1):
    return jax.nn.softmax(x, axis=axis)

def _gelu(x):
    return jax.nn.gelu(x, approximate=True)

def _silu(x):
    return jax.nn.silu(x)

def _sigmoid(x):
    return jax.nn.sigmoid(x)

def _layernorm(x, axis=-1, eps=1e-05):
    m = jnp.mean(x, axis=axis, keepdims=True)
    v = jnp.var(x, axis=axis, keepdims=True)
    return (x - m) / jnp.sqrt(v + eps)

def _scatter_add(tgt, idx, src, axis=0):
    return tgt.at[idx].add(src)

def _segment_sum(src, seg, n):
    return jax.ops.segment_sum(src, seg, n)
kernel_name = 'mk_early_fusion_d1_tok_img768_r4_c4f79b'

def setup_inputs(seed: int=0):
    np.random.seed(seed)
    _w = jnp.asarray

    def _rec_inputs():
        import jax
        import jax.numpy as jnp
        _rk = jax.random.key(seed)
        x = -0.000137204 + 0.999937 * jax.random.normal(jax.random.fold_in(_rk, 1), (4, 3, 96, 96), jnp.float32)
        txt = -0.000439578 + 0.0402453 * jax.random.normal(jax.random.fold_in(_rk, 2), (4, 512, 192), jnp.float32)
        return (x, txt)
    x, txt = _rec_inputs()

    def _L0_tok_setup():
        import jax, jax.numpy as jnp
        import numpy as np
        B, C, H, W_IMG = (128, 3, 224, 224)
        N_PATCH, EMBED = (256, 192)
        GRID = 32
        key = jax.random.key(seed)
        k1, k2, k3, k4 = jax.random.split(key, 4)
        x = jax.random.normal(k1, (B, C, H, W_IMG), dtype=jnp.float32)
        curve = jax.random.randint(k2, (N_PATCH, 2), 0, GRID, dtype=jnp.int32)
        proj_w = jax.random.normal(k3, (EMBED, C), dtype=jnp.float32) * 0.02
        proj_b = jax.random.normal(k4, (EMBED,), dtype=jnp.float32) * 0.02
        return {'x': x, 'curve': curve, 'proj_w': proj_w, 'proj_b': proj_b}
    _L0_tok_all = _L0_tok_setup()
    _L0_tok_in = {k: v for k, v in _L0_tok_all.items() if k in ('curve', 'proj_w', 'proj_b')}
    del _L0_tok_all

    def _L0_attn_setup():
        import jax, jax.numpy as jnp
        import numpy as np
        D_MODEL = 192
        H = 6
        DQK = 128
        DV = 64
        SCALE_BASE = 512.0

        def _xpos(x, sign):
            B, T, Hn, d = x.shape
            half = d // 2
            pos = jnp.arange(T, dtype=jnp.float32)
            inv_freq = 1.0 / 10000.0 ** (jnp.arange(half, dtype=jnp.float32) / half)
            angles = pos[:, None] * inv_freq[None, :]
            zeta = (jnp.arange(half, dtype=jnp.float32) + half) / d
            decay = zeta[None, :] ** (sign * pos[:, None] / SCALE_BASE)
            cos_a = (jnp.cos(angles) * decay)[None, :, None, :]
            sin_a = (jnp.sin(angles) * decay)[None, :, None, :]
            x1, x2 = (x[..., :half], x[..., half:])
            return jnp.concatenate([x1 * cos_a - x2 * sin_a, x1 * sin_a + x2 * cos_a], axis=-1)

        def _decay_mask(T):
            gammas = jnp.array([1.0 - 2.0 ** (-(5 + h)) for h in range(H)], dtype=jnp.float32)
            i = jnp.arange(T, dtype=jnp.float32)
            diff = i[:, None] - i[None, :]
            causal = (diff >= 0).astype(jnp.float32)
            D = gammas[:, None, None] ** jnp.clip(diff, 0.0)[None] * causal[None]
            row = jnp.clip(jnp.sum(D, axis=-1, keepdims=True), 1e-06)
            return D / jnp.sqrt(row)
        key = jax.random.key(seed)
        ks = jax.random.split(key, 6)
        B, T = (2, 512)

        def xavier(k, shape):
            lim = float(np.sqrt(6.0 / (shape[0] + shape[1])))
            return jax.random.uniform(k, shape, jnp.float32, -lim, lim)
        return {'x': jax.random.normal(ks[0], (B, T, D_MODEL), jnp.float32), 'Wq': xavier(ks[1], (D_MODEL, H * DQK)), 'Wk': xavier(ks[2], (D_MODEL, H * DQK)), 'Wv': xavier(ks[3], (D_MODEL, H * DV)), 'Wg': xavier(ks[4], (D_MODEL, H * DV)), 'Wo': xavier(ks[5], (H * DV, D_MODEL)), 'gn_weight': jnp.ones((H * DV,), jnp.float32), 'gn_bias': jnp.zeros((H * DV,), jnp.float32)}
    _L0_attn_all = _L0_attn_setup()
    _L0_attn_in = {k: v for k, v in _L0_attn_all.items() if k in ('Wq', 'Wk', 'Wv', 'Wg', 'Wo', 'gn_weight', 'gn_bias')}
    del _L0_attn_all

    def _L0_ffn_setup():
        import jax, jax.numpy as jnp
        import numpy as np
        B, T, D = (2, 512, 192)
        S, R, M, K = (8, 16, 64, 4)
        H, G = (32, 64)

        def _ssinf3(x, P, C, W1, b1, W2, b2, G1, g1b, G2, g2b):
            shp = x.shape
            xf = x.reshape(-1, shp[-1])
            z = jnp.einsum('nd,sdr->nsr', xf, P)
            scores = jnp.einsum('nsr,smr->nsm', z, C)
            topv, topi = jax.lax.top_k(scores, K)
            w = jax.nn.softmax(topv, axis=-1)
            sidx = jnp.arange(S)[None, :, None]
            W1g = W1[sidx, topi]
            b1g = b1[sidx, topi]
            W2g = W2[sidx, topi]
            b2g = b2[sidx, topi]
            h = jax.nn.gelu(jnp.einsum('nsr,nskrh->nskh', z, W1g) + b1g)
            yl = jnp.einsum('nskh,nskhr->nskr', h, W2g) + b2g
            comb = jnp.einsum('nskr,nsk->nsr', yl, w)
            comb = comb.reshape(xf.shape[0], S * R)
            out = jax.nn.gelu(comb @ G1 + g1b) @ G2 + g2b
            return out.reshape(shp)
        key = jax.random.key(seed)
        k = jax.random.split(key, 8)
        rn = lambda kk, shape, s: jax.random.normal(kk, shape, dtype=jnp.float32) * s
        return {'x': rn(k[0], (B, T, D), 1.0), 'P': rn(k[1], (S, D, R), D ** (-0.5)), 'C': rn(k[2], (S, M, R), R ** (-0.5)), 'W1': rn(k[3], (S, M, R, H), R ** (-0.5)), 'b1': jnp.zeros((S, M, H), jnp.float32), 'W2': rn(k[4], (S, M, H, R), H ** (-0.5)), 'b2': jnp.zeros((S, M, R), jnp.float32), 'G1': rn(k[5], (S * R, G), (S * R) ** (-0.5)), 'g1b': jnp.zeros((G,), jnp.float32), 'G2': rn(k[6], (G, D), G ** (-0.5)), 'g2b': jnp.zeros((D,), jnp.float32)}
    _L0_ffn_all = _L0_ffn_setup()
    _L0_ffn_in = {k: v for k, v in _L0_ffn_all.items() if k in ('P', 'C', 'W1', 'b1', 'W2', 'b2', 'G1', 'g1b', 'G2', 'g2b')}
    del _L0_ffn_all
    return {'x': x, 'txt': txt, 'L0_tok_curve': _L0_tok_in['curve'], 'L0_tok_proj_w': _L0_tok_in['proj_w'], 'L0_tok_proj_b': _L0_tok_in['proj_b'], 'L0_attn_Wq': _L0_attn_in['Wq'], 'L0_attn_Wk': _L0_attn_in['Wk'], 'L0_attn_Wv': _L0_attn_in['Wv'], 'L0_attn_Wg': _L0_attn_in['Wg'], 'L0_attn_Wo': _L0_attn_in['Wo'], 'L0_attn_gn_weight': _L0_attn_in['gn_weight'], 'L0_attn_gn_bias': _L0_attn_in['gn_bias'], 'L0_ffn_P': _L0_ffn_in['P'], 'L0_ffn_C': _L0_ffn_in['C'], 'L0_ffn_W1': _L0_ffn_in['W1'], 'L0_ffn_b1': _L0_ffn_in['b1'], 'L0_ffn_W2': _L0_ffn_in['W2'], 'L0_ffn_b2': _L0_ffn_in['b2'], 'L0_ffn_G1': _L0_ffn_in['G1'], 'L0_ffn_g1b': _L0_ffn_in['g1b'], 'L0_ffn_G2': _L0_ffn_in['G2'], 'L0_ffn_g2b': _L0_ffn_in['g2b']}

def reference(x, txt, L0_tok_curve, L0_tok_proj_w, L0_tok_proj_b, L0_attn_Wq, L0_attn_Wk, L0_attn_Wv, L0_attn_Wg, L0_attn_Wo, L0_attn_gn_weight, L0_attn_gn_bias, L0_ffn_P, L0_ffn_C, L0_ffn_W1, L0_ffn_b1, L0_ffn_W2, L0_ffn_b2, L0_ffn_G1, L0_ffn_g1b, L0_ffn_G2, L0_ffn_g2b):
    import jax
    import jax.numpy as jnp

    def _L0_tok_ref(x, curve, proj_w, proj_b):
        import jax, jax.numpy as jnp
        import numpy as np
        B, C, H, W_IMG = (128, 3, 224, 224)
        N_PATCH, EMBED = (256, 192)
        GRID = 32
        gathered = x[:, :, curve[:, 1], curve[:, 0]]
        return jnp.einsum('bcn,ec->bne', gathered, proj_w) + proj_b

    def _L0_attn_ref(x, Wq, Wk, Wv, Wg, Wo, gn_weight, gn_bias):
        import jax, jax.numpy as jnp
        import numpy as np
        D_MODEL = 192
        H = 6
        DQK = 128
        DV = 64
        SCALE_BASE = 512.0

        def _xpos(x, sign):
            B, T, Hn, d = x.shape
            half = d // 2
            pos = jnp.arange(T, dtype=jnp.float32)
            inv_freq = 1.0 / 10000.0 ** (jnp.arange(half, dtype=jnp.float32) / half)
            angles = pos[:, None] * inv_freq[None, :]
            zeta = (jnp.arange(half, dtype=jnp.float32) + half) / d
            decay = zeta[None, :] ** (sign * pos[:, None] / SCALE_BASE)
            cos_a = (jnp.cos(angles) * decay)[None, :, None, :]
            sin_a = (jnp.sin(angles) * decay)[None, :, None, :]
            x1, x2 = (x[..., :half], x[..., half:])
            return jnp.concatenate([x1 * cos_a - x2 * sin_a, x1 * sin_a + x2 * cos_a], axis=-1)

        def _decay_mask(T):
            gammas = jnp.array([1.0 - 2.0 ** (-(5 + h)) for h in range(H)], dtype=jnp.float32)
            i = jnp.arange(T, dtype=jnp.float32)
            diff = i[:, None] - i[None, :]
            causal = (diff >= 0).astype(jnp.float32)
            D = gammas[:, None, None] ** jnp.clip(diff, 0.0)[None] * causal[None]
            row = jnp.clip(jnp.sum(D, axis=-1, keepdims=True), 1e-06)
            return D / jnp.sqrt(row)
        B, T, _ = x.shape
        Q = (x @ Wq).reshape(B, T, H, DQK)
        K = (x @ Wk).reshape(B, T, H, DQK)
        V = (x @ Wv).reshape(B, T, H, DV)
        Q = _xpos(Q, 1.0)
        K = _xpos(K, -1.0)
        scores = jnp.einsum('bihd,bjhd->bhij', Q, K) * DQK ** (-0.5)
        scores = scores * _decay_mask(T)[None]
        out = jnp.einsum('bhij,bjhv->bihv', scores, V)
        concat = out.reshape(B, T, H * DV)
        g = concat.transpose(0, 2, 1).reshape(B, H, DV, T)
        mean = jnp.mean(g, axis=(2, 3), keepdims=True)
        var = jnp.var(g, axis=(2, 3), keepdims=True)
        g = (g - mean) / jnp.sqrt(var + 1e-05)
        g = g.reshape(B, H * DV, T) * gn_weight[None, :, None] + gn_bias[None, :, None]
        normed = g.transpose(0, 2, 1)
        gate = jax.nn.silu(x @ Wg)
        return normed * gate @ Wo

    def _L0_ffn_ref(x, P, C, W1, b1, W2, b2, G1, g1b, G2, g2b):
        import jax, jax.numpy as jnp
        import numpy as np
        B, T, D = (2, 512, 192)
        S, R, M, K = (8, 16, 64, 4)
        H, G = (32, 64)

        def _ssinf3(x, P, C, W1, b1, W2, b2, G1, g1b, G2, g2b):
            shp = x.shape
            xf = x.reshape(-1, shp[-1])
            z = jnp.einsum('nd,sdr->nsr', xf, P)
            scores = jnp.einsum('nsr,smr->nsm', z, C)
            topv, topi = jax.lax.top_k(scores, K)
            w = jax.nn.softmax(topv, axis=-1)
            sidx = jnp.arange(S)[None, :, None]
            W1g = W1[sidx, topi]
            b1g = b1[sidx, topi]
            W2g = W2[sidx, topi]
            b2g = b2[sidx, topi]
            h = jax.nn.gelu(jnp.einsum('nsr,nskrh->nskh', z, W1g) + b1g)
            yl = jnp.einsum('nskh,nskhr->nskr', h, W2g) + b2g
            comb = jnp.einsum('nskr,nsk->nsr', yl, w)
            comb = comb.reshape(xf.shape[0], S * R)
            out = jax.nn.gelu(comb @ G1 + g1b) @ G2 + g2b
            return out.reshape(shp)
        return _ssinf3(x, P, C, W1, b1, W2, b2, G1, g1b, G2, g2b)
    h = _L0_tok_ref(x, L0_tok_curve, L0_tok_proj_w, L0_tok_proj_b)
    h = jnp.concatenate([h, txt], axis=1)
    h = h + _L0_attn_ref(_layernorm(h, axis=-1), L0_attn_Wq, L0_attn_Wk, L0_attn_Wv, L0_attn_Wg, L0_attn_Wo, L0_attn_gn_weight, L0_attn_gn_bias)
    h = h + _L0_ffn_ref(_layernorm(h, axis=-1), L0_ffn_P, L0_ffn_C, L0_ffn_W1, L0_ffn_b1, L0_ffn_W2, L0_ffn_b2, L0_ffn_G1, L0_ffn_g1b, L0_ffn_G2, L0_ffn_g2b)
    return h

_drawn_inputs = setup_inputs


def setup_inputs(seed=0):
    import zlib

    import numpy as np

    out = dict(_drawn_inputs(seed))
    spreads = {'L0_attn_gn_weight': (1.0, 0.2),
     'L0_attn_gn_bias': (0.0, 0.1),
     'L0_ffn_b1': (0.0, 0.1),
     'L0_ffn_b2': (0.0, 0.1),
     'L0_ffn_g1b': (0.0, 0.1),
     'L0_ffn_g2b': (0.0, 0.1)}
    factors = {}
    for name, (base, spread) in spreads.items():
        noise = np.random.default_rng([zlib.crc32(name.encode()), seed]).standard_normal(out[name].shape)
        drawn = base * np.exp(spread * noise) if base else spread * noise
        out[name] = jnp.asarray(drawn.astype(out[name].dtype))
    for name, factor in factors.items():
        out[name] = (out[name] * factor).astype(out[name].dtype)
    return out
```

```python
from contextlib import ExitStack

import concourse.bass as bass
from concourse import mybir

F32 = mybir.dt.float32
BF16 = mybir.dt.bfloat16
I32 = mybir.dt.int32
ALU = mybir.AluOpType
ACT = mybir.ActivationFunctionType
AXX = mybir.AxisListType.X

P = 128
B, CIN, IMG = 4, 3, 96
NPATCH, TXT, D = 256, 512, 192
D2 = D - P
T = NPATCH + TXT
CH = T // P
TILES = B * CH
PAIRS = TILES // 2
H, DQK, DV = 6, 128, 64
QK = H * DQK
HV = H * DV
VP = HV // P
S, R, M, TOPK, HID, GH = 8, 16, 64, 4, 32, 64
BLK = 512
NBLK = B * T // BLK
NIT = NBLK * 4
LEAD = 5
LENT = 1
UNITS = 32
TAKEN = -2.0 ** 100
FILLER = -2.0 ** 101
EPS = 1e-5


def ds(start, size):
    return bass.ds(start, size)


def fused_layer(nc, t):
    out = t["out"]
    w1_parts = nc.dram_tensor("w1_parts", (3, P, M * HID), BF16, kind="Internal").ap()
    b1_parts = nc.dram_tensor("b1_parts", (3, P, P), BF16, kind="Internal").ap()
    z_parts = nc.dram_tensor("z_parts", (3, P, B * T), BF16, kind="Internal").ap()
    w_parts = nc.dram_tensor("w_parts", (3, S * M, B * T), BF16, kind="Internal").ap()

    with ExitStack() as ctx:
        def alloc(stack, name, shape, dt=F32):
            return stack.enter_context(nc.sbuf_tensor(name, shape, dt))

        def sb(name, shape, dt=F32):
            return alloc(ctx, name, shape, dt)

        def sem(name):
            return ctx.enter_context(nc.semaphore(name))

        h = sb("h", [P, TILES + 2, D])
        ident = sb("ident", [P, P])
        stats = sb("stats", [P, TILES + 2, 6])
        mean = sb("mean", [P, TILES + 2])
        rstd = sb("rstd", [P, TILES + 2])
        gns = sb("gns", [P, TILES, VP, 6])
        lns = sb("lns", [P, 4, TILES + 2])

        with ExitStack() as region:
            oT = alloc(region, "oT", [P, TILES, VP, P])
            gate = alloc(region, "gate", [P, TILES, VP, P])
        with ExitStack() as region:
            ring = alloc(region, "ring", [P, 8, BLK])
            ysum = alloc(region, "ysum", [P, 13, BLK])
            zst = alloc(region, "zst", [P, 2, 4, BLK], BF16)
            wst = alloc(region, "wst", [P, 2, 4, BLK], BF16)
            sc = alloc(region, "sc", [P, S, M + 4])
            mr = alloc(region, "mr", [P, S, M + 4])
            dist = alloc(region, "dist", [P, S * M + S * TOPK])
            taken = alloc(region, "taken", [P, S, M])
            wn = alloc(region, "wn", [P, S, M])
        gap = ctx.enter_context(nc.sbuf_tensor("region_one", [P, 2 * TILES * VP * P], F32))

        with ExitStack() as region:
            wcat = alloc(region, "wcat", [P, 2, 2 * QK + 2 * HV])
            rope = alloc(region, "rope", [P, CH, 4, P])
            oscale = alloc(region, "oscale", [P, CH, VP, P])
            vscale = alloc(region, "vscale", [P, CH, H])
            causal = alloc(region, "causal", [P, P])
            t1 = alloc(region, "t1", [P, 4, H, DQK])
            t2 = alloc(region, "t2", [P, 4, H, DQK])
            qkT = alloc(region, "qkT", [P, 4, H, P])
            pT = alloc(region, "pT", [P, 2, H, P])
            vn = alloc(region, "vn", [P, 2, H, DV])
            state = alloc(region, "state", [P, 2, H, DV])
            xn = alloc(region, "xn", [P, 2, D])
            xnT = alloc(region, "xnT", [P, 2, 2, P])
            xim = t1[0:IMG, 0:2, :, :].rearrange("p a h d -> p (a h d)")[:, 0:B * CIN * IMG]
            picked = t2[:, 0:2, :, :].rearrange("p a h d -> p (a h d)")[:, 0:B * CIN * IMG]
            curve_bc = alloc(region, "curve_bc", [IMG, NPATCH, 2], I32)
            curve_n = alloc(region, "curve_n", [P, 2, 2], I32)
            curve_f = alloc(region, "curve_f", [P, 2, 2])
            iota_p = alloc(region, "iota_p", [P, 1])
            iota_x = alloc(region, "iota_x", [P, IMG])
            row_hot = alloc(region, "row_hot", [IMG, NPATCH])
            col_hot = alloc(region, "col_hot", [P, 2, IMG])
            pix = alloc(region, "pix", [P, 2, B * CIN + 1])
            pixT = alloc(region, "pixT", [B * CIN + 1, 2, P])
            wblk = alloc(region, "wblk", [B * CIN + 1, B * D])
        w1st = sb("w1st", [P, S, M * HID], BF16)
        zT = sb("zT", [P, B * T])
        w2cur = sb("w2cur", [P, 8, 4, 32])
        b2w = sb("b2w", [P, 4, P])
        sel = sb("sel", [96, 8, P], BF16)
        cblk = sb("cblk", [P, S * M])
        pw = sb("pw", [P, 2, P])
        g1 = sb("g1", [P, 2, GH])
        g1b = sb("g1b", [GH, 1])
        g2 = sb("g2", [GH + 1, D])
        uT = sb("uT", [GH + 1, BLK])
        wo = sb("wo", [P, VP, D])
        gnw = sb("gnw", [P, VP])
        gnb = sb("gnb", [P, VP])
        halves = sb("halves", [P, P])
        gmv = sb("gmv", [P, B, VP, 2])
        gtmp = sb("gtmp", [P, 6, B, VP])
        gscale = sb("gscale", [P, B, VP])
        gbias = sb("gbias", [P, B, VP])
        yg = sb("yg", [P, 2, VP, P])
        zcur = sb("zcur", [P, P])
        carrier = sb("carrier", [P, 1])
        act_carrier = sb("act_carrier", [P, 1])
        top8 = sb("top8", [P, S, 8])
        top4 = sb("top4", [P, S, TOPK])
        norm = sb("norm", [P, 2, S])
        wp = sb("wp", [P, 3, 4, P], BF16)
        wr = sb("wr", [P, 4, P])
        wT = sb("wT", [P, 4, P])
        w1f = sb("w1f", [P, M * HID])
        w1p = sb("w1p", [P, 3, M * HID], BF16)
        b1f = sb("b1f", [P, P])
        b1p = sb("b1p", [P, 3, P], BF16)
        zp = sb("zp", [P, 3, BLK], BF16)
        zr = sb("zr", [P, BLK])
        x2 = sb("x2", [P, 4, D])
        x2T = sb("x2T", [P, 2, BLK])
        del gap

        ps = ctx.enter_context(nc.psum_tensor("ps", [P, 8 * 512], F32))

        def bank(n, a=0, b=512, p0=0, p1=P):
            return ps[p0:p1, n * 512 + a:n * 512 + b]

        block = ctx.enter_context(nc.Block())
        names = ("ld_img ld_text ld_attn ld_late ld_w1 ld_scr st_w1 st_z zero hot seen picked_s pix_t pixt_s img image "
                 "st1 ln_var ln_std ln_done xn_d xn_t xn_e "
                 "q0 q1 k0 k1 v0 v1 g0 g1s rq0 rq1 rk0 rk1 ve0 ve1 ge0 ge1 aq0 aq1 ak0 ak1 tq0 tq1 tk0 tk1 "
                 "eq0 eq1 ek0 ek1 sc0 sc1 m0 m1 st0s st1s o0 o1 oe0 oe1 se0 se1 reset dchain "
                 "gn_in gn_m gn_dev gn_v gn_std gn_done yn yg_d wo_s res "
                 "x2_d x2_t x2_e z_s z_hi z_r z_mid z_lo b_hi b_r b_mid "
                 "a_full a_free w_full w_free w2_done y_done y_kept zc s_full s_copied t_top t_mr p_dist p_taken e_done "
                 "n_done p_em p_w t_full hi_done r_done mid_done lo_done w_stored stack w2_lo w2_hi wT_done b2_full y_begun sel_cast "
                 "ready fin_y fin_u fin_g fin_o fin_h stored").split()
        s = {n: sem(n) for n in names}
        lent = ("oe0 se0 oe1 se1 m0 m1 o0 o1 aq0 aq1 ak0 ak1 x2_e x2_t z_s res wo_s y_begun "
                "t_mr p_dist p_taken b2_full w_stored st_z fin_o fin_h s_full p_w lo_done t_full p_em n_done w2_done y_kept w_full xn_t").split()

        def attention_over(eng):
            for n in ("oe0", "oe1", "se0", "se1", "ge0", "ge1", "xn_e"):
                eng.wait_ge(s[n], PAIRS + (n == "xn_e") + LENT * (n in lent))

        def settle(eng):
            eng.wait_ge(s["ready"], 1)

        @block.sync
        def _(sp):
            sp.dma_start(curve_bc[:, :, :], _bcast(t["curve"], IMG)).then_inc(s["ld_img"], 16)
            sp.dma_start(curve_n[:, :, :], t["curve"].rearrange("(n p) c -> p n c", p=P)).then_inc(s["ld_img"], 16)
            sp.dma_start(iota_p[:, :], t["iota_p"]).then_inc(s["ld_img"], 16)
            sp.dma_start(iota_x[:, :], t["iota_x"]).then_inc(s["ld_img"], 16)
            sp.dma_start(xim.rearrange("p (n x) -> p n x", x=IMG),
                         t["x"].rearrange("b c y x -> y (b c) x")).then_inc(s["ld_img"], 16)
            sp.dma_start(wblk[:, :], t["wblk"]).then_inc(s["ld_img"], 16)
            sp.dma_start(ident[:, :], t["ident"]).then_inc(s["ld_img"], 16)
            for b in range(B):
                first = 12 * (b // 2) + 4 + b % 2
                sp.dma_start(h[:, first:first + 7:2, :],
                             t["txt"][b].rearrange("(c p) e -> p c e", p=P)).then_inc(s["ld_text"], 16)
            sp.dma_start(wcat[:, 0, :], t["wcat"][0:P, :]).then_inc(s["ld_attn"], 16)
            sp.dma_start(wcat[0:D2, 1, :], t["wcat"][P:D, :]).then_inc(s["ld_attn"], 16)
            sp.dma_start(rope[:, :, :, :], t["rope"]).then_inc(s["ld_attn"], 16)
            sp.dma_start(oscale[:, :, :, :], t["oscale"]).then_inc(s["ld_attn"], 16)
            sp.dma_start(vscale[:, :, :], t["vscale"]).then_inc(s["ld_attn"], 16)
            sp.dma_start(causal[:, :], t["causal"]).then_inc(s["ld_attn"], 16)
            attention_over(sp)
            sp.dma_start(w1f[:, :], t["w1"]).then_inc(s["ld_w1"], 16)
            sp.dma_start(b1f[:, :], t["b1"]).then_inc(s["ld_w1"], 16)
            for dst, src in ((halves[:, :], t["halves"]), (gnw[:, :], t["gnw"]), (gnb[:, :], t["gnb"]),
                             (wo[:, :, :], t["wo"].rearrange("(c p) e -> p c e", p=P)),
                             (pw[:, 0, :], t["pw"][0:P, :]), (pw[0:D2, 1, :], t["pw"][P:D, :]),
                             (cblk[:, :], t["cblk"]), (b2w[:, :, :], t["b2"]), (x2T[0:96, :, :], t["sel"]), (g1[:, :, :], t["g1"]),
                             (g1b[:, :], t["g1b"]), (g2[:, :], t["g2"])):
                sp.dma_start(dst, src).then_inc(s["ld_late"], 16)
            sp.wait_ge(s["z_lo"], 1)
            for k in range(3):
                sp.dma_start(w1_parts[k], w1p[:, k, :]).then_inc(s["st_w1"], 16)
                sp.dma_start(b1_parts[k], b1p[:, k, :]).then_inc(s["st_w1"], 16)
            sp.wait_ge(s["st_w1"], 96)
            for n, k in enumerate((0, 1, 0, 2, 0, 1)):
                sp.dma_start(w1st[R * n:R * n + R, :, :],
                             w1_parts[k].rearrange("(s r) n -> r s n", r=R)).then_inc(s["ld_scr"], 16)
            for k in range(3):
                sp.dma_start(w1st[96 + k:97 + k, :, :],
                             b1_parts[k].rearrange("(o s a) n -> o s (a n)", o=1, s=S)).then_inc(s["ld_scr"], 16)
            with sp.Fori(0, NBLK) as i:
                sp.wait_ge(s["z_lo"], i + 2)
                sp.dma_start(z_parts[:, :, ds(i * BLK, BLK)].rearrange("k p n -> p k n"),
                             zp[:, :, :]).then_inc(s["st_z"], 16)
            sp.wait_ge(s["st_z"], LENT + 16 * NBLK)

            def store_gates(tile):
                sp.wait_ge(s["lo_done"], LENT + tile + 1)
                for k in range(3):
                    sp.dma_start(w_parts[k, :, ds(tile * P, P)].rearrange("(g p) n -> p g n", p=P),
                                 wp[:, k, :, :]).then_inc(s["w_stored"], 16)

            def load_stack(i, par, blk, a, kt):
                for n, k in enumerate((0, 0, 1, 0, 2, 1)):
                    sp.dma_start(zst[R * n:R * n + R, ds(par, 1), :, :].rearrange("p o j n -> p (o j) n"),
                                 z_parts[k, ds(a * (4 * R), 4 * R), ds(blk * BLK, BLK)]
                                 .rearrange("(j r) n -> r j n", r=R)).then_inc(s["stack"], 16)
                for k in range(3):
                    sp.dma_start(wst[32 * k:32 * k + 32, ds(par, 1), :, :].rearrange("p o j n -> p (o j) n"),
                                 _gate_rows(w_parts, k, a, kt, blk)).then_inc(s["stack"], 16)

            def load_w2(i, combo, half):
                sp.dma_start(w2cur[:, 4 * half:4 * half + 4, :, :].rearrange("p q j r -> p (q j r)"),
                             t["w2"][ds(combo, 1), :, 512 * half:512 * half + 512]
                             .rearrange("o p n -> (o p) n")).then_inc(s["w2_hi" if half else "w2_lo"], 16)

            with sp.Fori(0, LEAD) as i:
                store_gates(i)
            sp.wait_ge(s["w_stored"], LENT + 48 * LEAD)
            sp.wait_ge(s["ready"], 1)
            load_stack(0, 0, 0, 0, 0)
            load_w2(0, 0, 0)

            def step(i, last=False, gates=True):
                sp.wait_ge(s["w2_done"], LENT + 8 * i + 1)
                load_w2(i, i % 4, 1)
                if not last:
                    sp.wait_ge(s["w_full"], LENT + UNITS * i)
                    sp.wait_ge(s["stack"], 144 * (i + 1))
                    sp.wait_ge(s["w_stored"], LENT + (48 * (i + LEAD) if gates else 48 * TILES))
                    n = i + 1
                    load_stack(n, n % 2, n // 4, (n // 2) % 2, n % 2)
                    sp.wait_ge(s["w2_done"], LENT + 8 * i + 5)
                    load_w2(n, n % 4, 0)

            with sp.Fori(0, NIT - LEAD) as i:
                step(i)
                store_gates(i + LEAD)
            with sp.Fori(NIT - LEAD, NIT - 1) as i:
                step(i, gates=False)
            step(NIT - 1, last=True)
            with sp.Fori(0, 2) as bb:
                with sp.Fori(0, 3) as cb:
                    blk = bb * 3 + cb
                    sp.wait_ge(s["fin_h"], LENT + blk + 1)
                    for x in range(2):
                        sp.dma_start(out[ds(bb * 2 + x, 1), ds(cb * 2 * P, 2 * P), :]
                                     .rearrange("o (k p) e -> p (o k) e", p=P),
                                     h[:, ds(blk * 4 + x, 3), :][:, 0:3:2, :]).then_inc(s["stored"], 16)
            sp.wait_ge(s["stored"], 16 * 2 * NBLK)

        @block.tensor
        def _(pe):
            pe.wait_ge(s["ld_img"], 16 * 7)
            pe.wait_ge(s["hot"], 1)
            for n in range(2):
                for k in range(3):
                    mm = pe.matmul(bank(3 * n + k, 0, 384), row_hot[:, n * P:n * P + P],
                                   xim[:, 384 * k:384 * k + 384], start=True, stop=True)
            mm.then_inc(s["seen"], 1)
            pe.wait_ge(s["picked_s"], 1)
            for n in range(2):
                mm = pe.transpose(bank(6, n * P, n * P + P, 0, B * CIN + 1), pix[:, n, :], ident[:, :])
            mm.then_inc(s["pix_t"], 1)
            pe.wait_ge(s["pixt_s"], 1)
            for n in range(2):
                for k in range(2):
                    mm = pe.matmul(bank(2 * n + k, 0, 384), pixT[:, n, :], wblk[:, 384 * k:384 * k + 384],
                                   start=True, stop=True)
            mm.then_inc(s["img"], 1)

            def xn_turn(n):
                pe.wait_ge(s["xn_d"], n + 1)
                for x in range(2):
                    pe.transpose(bank(4, x * P, x * P + P), xn[:, x, 0:P], ident[:, :])
                    mm = pe.transpose(bank(4, (2 + x) * P, (3 + x) * P, 0, D2), xn[:, x, P:D], ident[:, :])
                mm.then_inc(s["xn_t"], 1)

            pe.wait_ge(s["image"], 1)
            xn_turn(0)
            pe.wait_ge(s["ld_attn"], 16 * 6)

            def wide(to, x, col, n, name):
                for a in range(0, n, 512):
                    w = min(512, n - a)
                    pe.matmul(bank(to + a // 512, 0, w), xnT[:, x, 0, :], wcat[:, 0, col + a:col + a + w],
                              start=True, stop=False)
                    mm = pe.matmul(bank(to + a // 512, 0, w), xnT[0:D2, x, 1, :], wcat[0:D2, 1, col + a:col + a + w],
                                   start=False, stop=True)
                mm.then_inc(s[name], 1)

            def values_gates(to, x):
                wide(to, x, 2 * QK, HV, f"v{x}")
                for g in range(VP):
                    col = 2 * QK + HV + g * P
                    pe.matmul(bank(to + 1, g * P, g * P + P), wcat[:, 0, col:col + P], xnT[:, x, 0, :],
                              start=True, stop=False)
                    mm = pe.matmul(bank(to + 1, g * P, g * P + P), wcat[0:D2, 1, col:col + P], xnT[0:D2, x, 1, :],
                                   start=False, stop=True)
                mm.then_inc(s["g0" if x == 0 else "g1s"], 1)

            def turn(to, src, name):
                for e in range(H):
                    mm = pe.transpose(ps[:, to * 512 + e * P:to * 512 + e * P + P], src[:, e, :], ident[:, :])
                mm.then_inc(s[name], 1)

            def heads(x, k, to_s):
                for e in range(H):
                    mm = pe.matmul(ps[:, to_s * 512 + e * P:to_s * 512 + e * P + P], qkT[:, 2 * x + 1, e, :],
                                   qkT[:, 2 * x, e, :], start=True, stop=True)
                mm.then_inc(s[f"sc{x}"], 1)

            def outputs(x, to):
                for e in range(H):
                    mm = pe.matmul(bank(to + 1, e * DV, e * DV + DV), t1[:, 2 * x + 1, e, :], vn[:, x, e, :],
                                   start=True, stop=True)
                mm.then_inc(s[f"st{x}s"], 1)
                for g in range(VP):
                    for part in range(2):
                        for e in range(2):
                            o = bank(to, g * P, g * P + P, e * DV, e * DV + DV)
                            if part == 0:
                                mm = pe.matmul(o, vn[:, x, 2 * g + e, :], pT[:, x, 2 * g + e, :], start=True, stop=False)
                            else:
                                mm = pe.matmul(o, state[:, x, 2 * g + e, :], qkT[:, 2 * x, 2 * g + e, :],
                                               start=False, stop=True)
                mm.then_inc(s[f"o{x}"], 1)

            with pe.Fori(0, 2) as bb:
                with pe.Fori(0, CH) as c:
                    k = bb * CH + c
                    pe.wait_ge(s["xn_e"], k + 1)
                    pe.wait_ge(s["oe0"], LENT + k)
                    pe.wait_ge(s["se0"], LENT + k)
                    wide(0, 0, 0, QK, "q0")
                    pe.wait_ge(s["oe1"], LENT + k)
                    pe.wait_ge(s["se1"], LENT + k)
                    wide(2, 0, QK, QK, "k0")
                    pe.wait_ge(s["m0"], LENT + k)
                    values_gates(4, 0)
                    pe.wait_ge(s["rq0"], k + 1)
                    wide(0, 1, 0, QK, "q1")
                    pe.wait_ge(s["rk0"], k + 1)
                    wide(2, 1, QK, QK, "k1")
                    pe.wait_ge(s["m1"], LENT + k)
                    values_gates(6, 1)
                    pe.wait_ge(s["ve0"], k + 1)
                    xn_turn(k + 1)
                    pe.wait_ge(s["ve1"], k + 1)
                    pe.wait_ge(s["ge1"], k + 1)
                    pe.wait_ge(s["ak0"], LENT + k + 1)
                    turn(6, t1[:, 1], "tk0")
                    pe.wait_ge(s["aq1"], LENT + k + 1)
                    turn(0, t1[:, 2], "tq1")
                    pe.wait_ge(s["xn_e"], k + 2)
                    pe.wait_ge(s["ge0"], k + 1)
                    pe.wait_ge(s["aq0"], LENT + k + 1)
                    turn(4, t1[:, 0], "tq0")
                    pe.wait_ge(s["ak1"], LENT + k + 1)
                    turn(2, t1[:, 3], "tk1")
                    pe.wait_ge(s["eq0"], k + 1)
                    pe.wait_ge(s["ek0"], k + 1)
                    heads(0, k, 4)
                    pe.wait_ge(s["eq1"], k + 1)
                    pe.wait_ge(s["ek1"], k + 1)
                    heads(1, k, 6)
                    pe.wait_ge(s["reset"], bb + 1)
                    pe.wait_ge(s["m0"], LENT + k + 1)
                    outputs(0, 0)
                    pe.wait_ge(s["m1"], LENT + k + 1)
                    outputs(1, 2)

            pe.wait_ge(s["ld_late"], 16 * 12)
            pe.wait_ge(s["gn_in"], 1)
            pe.matmul(bank(0, 0, 24), halves[:, :], gmv[:, :, :, :].rearrange("p b g k -> p (b g k)"),
                      start=True, stop=True).then_inc(s["gn_m"], 1)
            pe.wait_ge(s["gn_dev"], 1)
            pe.matmul(bank(1, 0, 12), halves[:, :], gtmp[:, 1, :, :].rearrange("p b g -> p (b g)"),
                      start=True, stop=True).then_inc(s["gn_v"], 1)
            with pe.Fori(0, PAIRS) as k:
                for x in range(2):
                    pe.wait_ge(s["yg_d"], k * 2 + x + 1)
                    pe.wait_ge(s["res"], LENT + k * 2)
                    for g in range(VP):
                        mm = pe.matmul(bank(2 + x, 0, D), yg[:, x, g, :], wo[:, g, :], start=(g == 0), stop=(g == VP - 1))
                    mm.then_inc(s["wo_s"], 1)
            with pe.Fori(0, NBLK) as i:
                pe.wait_ge(s["x2_d"], i + 1)
                pe.wait_ge(s["x2_e"], LENT + i)
                for n in range(4):
                    pe.transpose(bank(4, n * P, n * P + P), x2[:, n, 0:P], ident[:, :])
                    mm = pe.transpose(bank(5, n * P, n * P + P, 0, D2), x2[:, n, P:D], ident[:, :])
                mm.then_inc(s["x2_t"], 1)
                pe.wait_ge(s["x2_e"], LENT + i + 1)
                pe.wait_ge(s["z_r"], i + 1)
                pe.matmul(bank(6), pw[:, 0, :], x2T[:, 0, :], start=True, stop=False)
                pe.matmul(bank(6), pw[0:D2, 1, :], x2T[0:D2, 1, :], start=False, stop=True).then_inc(s["z_s"], 1)

            def scores(tile):
                pe.wait_ge(s["y_begun"], LENT + tile)
                pe.wait_ge(s["zc"], tile + 1)
                pe.matmul(bank(7), zcur[:, :], cblk[:, :], start=True, stop=True).then_inc(s["s_full"], 1)

            def turn_gates(tile):
                pe.wait_ge(s["p_w"], LENT + tile + 1)
                for g in range(4):
                    mm = pe.transpose(bank(7, g * P, g * P + P),
                                      wn[:, 2 * g:2 * g + 2, :].rearrange("p s m -> p (s m)"), ident[:, :])
                mm.then_inc(s["t_full"], 1)

            def gated_b2(tile):
                pe.wait_ge(s["wT_done"], tile + 1)
                pe.wait_ge(s["r_done"], tile + 1)
                for a in range(2):
                    for g in range(2):
                        mm = pe.matmul(bank(7, a * P, a * P + P), b2w[:, 2 * a + g, :], wT[:, 2 * a + g, :],
                                       start=(g == 0), stop=(g == 1))
                mm.then_inc(s["b2_full"], 1)

            pe.wait_ge(s["z_r"], NBLK + 1)
            with pe.Fori(0, LEAD) as i:
                scores(i)
                turn_gates(i)
                gated_b2(i)

            pe.wait_ge(s["ready"], 1)
            pe.wait_ge(s["sel_cast"], 1)
            pe.matmul(bank(6), sel[0:96, 0, :], zst[0:96, 1, 0, :], start=True, stop=True)
            pe.wait_ge(s["ld_scr"], 16 * 9)

            def second(n, i, u0, wait):
                pe.wait_ge(s["w_free"], wait + 2)
                for j in range(4):
                    mm = pe.matmul(bank(6, 0, 512, 32 * j, 32 * j + 32), w2cur[:, n, j, :], ring[:, (4 * n + j) % 8, :],
                                   start=(n == 0), stop=(n == 7), skip_group_check=True)
                mm.then_inc(s["w2_done"], 1)
                return mm

            def iteration(i, prep):
                par = i % 2
                a = (i // 2) % 2
                base = a * (4 * M * HID) + par * (32 * HID)
                pe.wait_ge(s["stack"], 144 * (i + 1))
                w1flat = w1st[:, :, :].rearrange("p s n -> p (s n)")
                zflat = zst[:, :, :, :].rearrange("p a j n -> p (a j n)")
                wflat = wst[:, :, :, :].rearrange("p a j n -> p (a j n)")
                for n in range(8):
                    for j in range(4):
                        u = 4 * n + j
                        pe.wait_ge(s["a_free"], UNITS * i + u + 1)
                        pe.matmul(bank(u % 4), w1flat[0:99, ds(base + j * (M * HID) + n * P, P)],
                                  zflat[0:99, ds(par * (4 * BLK) + j * BLK, BLK)],
                                  start=True, stop=True).then_inc(s["a_full"], 1)
                        pe.wait_ge(s["w_free"], UNITS * i + u + 1)
                        pe.matmul(bank(4 + u % 2), sel[:, n, :],
                                  wflat[0:96, ds(par * (4 * BLK) + j * BLK, BLK)],
                                  start=True, stop=True).then_inc(s["w_full"], 1)
                    if n == 0:
                        second(7, i, 28, UNITS * i)
                    else:
                        if n == 1:
                            pe.wait_ge(s["y_kept"], LENT + i + 1)
                            pe.wait_ge(s["w2_lo"], 16 * (i + 1))
                        if n == 5:
                            pe.wait_ge(s["w2_hi"], 16 * (i + 1))
                        second(n - 1, i, 4 * (n - 1), UNITS * i + 4 * n)
                    if prep and n == 1:
                        scores(i + LEAD)
                    if prep and n == 6:
                        turn_gates(i + LEAD)
                    if prep and n == 7:
                        gated_b2(i + LEAD)

            with pe.Fori(0, NIT - LEAD) as i:
                iteration(i, True)
            with pe.Fori(NIT - LEAD, NIT) as i:
                iteration(i, False)
            second(7, NIT, 28, UNITS * NIT)
            with pe.Fori(0, NBLK) as i:
                pe.wait_ge(s["fin_y"], i + 1)
                for a in range(2):
                    mm = pe.matmul(bank(0, 0, 512, 0, GH), g1[:, a, :], ysum[:, ds(i * 2 + a + 1, 1), :]
                                   .rearrange("p o n -> p (o n)"), start=(a == 0), stop=(a == 1))
                mm.then_inc(s["fin_u"], 1)
                pe.wait_ge(s["fin_g"], i + 1)
                pe.wait_ge(s["fin_h"], LENT + i)
                for n in range(4):
                    mm = pe.matmul(bank(1 + n, 0, D), uT[:, n * P:n * P + P], g2[:, :], start=True, stop=True)
                mm.then_inc(s["fin_o"], 1)

        @block.scalar
        def _(act):
            act.wait_ge(s["pix_t"], 1)
            act.copy(pixT[:, :, :], bank(6, 0, 2 * P, 0, B * CIN + 1).rearrange("p (n t) -> p n t", n=2)).then_inc(s["pixt_s"], 1)
            act.wait_ge(s["img"], 1)
            for n in range(2):
                for k in range(2):
                    mm = act.copy(h[:, 12 * k + 2 * n:12 * k + 2 * n + 2, :],
                                  bank(2 * n + k, 0, 384).rearrange("p (b e) -> p b e", b=2))
            mm.then_inc(s["image"], 1)
            act.wait_ge(s["ln_var"], 1)
            act.activation(lns[:, 3, :], lns[:, 2, :], ACT.Sqrt).then_inc(s["ln_std"], 1)

            def xn_out(n):
                act.wait_ge(s["xn_t"], LENT + n + 1)
                act.copy(xnT[:, :, 0, :], bank(4, 0, 2 * P).rearrange("p (x n) -> p x n", x=2))
                act.copy(xnT[0:D2, :, 1, :], bank(4, 2 * P, 4 * P, 0, D2)
                         .rearrange("p (x n) -> p x n", x=2)).then_inc(s["xn_e"], 1)

            xn_out(0)
            with act.Fori(0, 2) as bb:
                with act.Fori(0, CH) as c:
                    k = bb * CH + c
                    for x in range(2):
                        act.wait_ge(s["g0" if x == 0 else "g1s"], k + 1)
                        act.activation(gate[:, ds(k * 2 + x, 1), :, :].rearrange("p o g n -> p (o g n)"),
                                       bank(5 + 2 * x, 0, 384), ACT.Silu).then_inc(s[f"ge{x}"], 1)
                    xn_out(k + 1)
                    for x, kind in ((0, 1), (1, 0), (0, 0), (1, 1)):
                        what = "qk"[kind]
                        act.wait_ge(s[f"t{what}{x}"], k + 1)
                        act.wait_ge(s[f"o{x}"], LENT + k)
                        to = (0 if x else 4) + 2 * kind
                        act.copy(qkT[:, 2 * x + kind, :, :].rearrange("p h n -> p (h n)"),
                                 ps[:, to * 512:to * 512 + QK]).then_inc(s[f"e{what}{x}"], 1)
            act.wait_ge(s["ld_w1"], 32)
            act.copy(w1p[:, 0, :], w1f[:, :])
            act.copy(b1p[:, 0, :], b1f[:, :]).then_inc(s["b_hi"], 1)
            act.wait_ge(s["b_r"], 1)
            act.copy(w1p[:, 1, :], w1f[:, :])
            act.copy(b1p[:, 1, :], b1f[:, :]).then_inc(s["b_mid"], 1)
            act.wait_ge(s["gn_std"], 1)
            act.activation(gtmp[:, 3, :, :], gtmp[:, 2, :, :], ACT.Sqrt).then_inc(s["gn_std"], 1)
            act.wait_ge(s["ld_late"], 16 * 12)
            act.copy(sel[:, :, :].rearrange("p q n -> p (q n)"), x2T[0:96, :, :].rearrange("p a n -> p (a n)")).then_inc(s["sel_cast"], 1)
            act.wait_ge(s["gn_done"], 1)
            with act.Fori(0, 2) as bb:
                with act.Fori(0, CH) as c:
                    k = bb * CH + c
                    for x in range(2):
                        act.wait_ge(s["wo_s"], LENT + k * 2)
                        for g in range(VP):
                            col = (bb * 2 + x) * VP + g
                            mm = act.activation(yg[:, x, g, :],
                                                oT[:, ds(k * 2 + x, 1), g, :].rearrange("p o n -> p (o n)"),
                                                ACT.Identity,
                                                bias=gbias[:, :, :].rearrange("p b g -> p (b g)")[:, ds(col, 1)],
                                                scale=gscale[:, :, :].rearrange("p b g -> p (b g)")[:, ds(col, 1)])
                        mm.then_inc(s["yn"], 1)
            act.wait_ge(s["ln_var"], 2)
            act.activation(lns[:, 3, :], lns[:, 2, :], ACT.Sqrt).then_inc(s["ln_std"], 1)
            with act.Fori(0, NBLK) as i:
                act.wait_ge(s["x2_t"], LENT + i + 1)
                act.wait_ge(s["sel_cast"], 1)
                act.wait_ge(s["z_s"], LENT + i)
                act.copy(x2T[:, 0, :], bank(4))
                act.copy(x2T[0:D2, 1, :], bank(5, 0, 512, 0, D2)).then_inc(s["x2_e"], 1)
                act.wait_ge(s["z_s"], LENT + i + 1)
                act.wait_ge(s["st_z"], LENT + 16 * i)
                act.copy(zT[:, ds(i * BLK, BLK)], bank(6))
                act.copy(zp[:, 0, :], bank(6)).then_inc(s["z_hi"], 1)
                act.wait_ge(s["z_r"], i + 2)
                act.copy(zp[:, 1, :], zr[:, :]).then_inc(s["z_mid"], 1)

            def copy_scores(tile):
                act.wait_ge(s["s_full"], LENT + tile + 1)
                act.wait_ge(s["p_taken"], LENT + tile)
                act.wait_ge(s["p_dist"], LENT + tile)
                act.copy(sc[:, :, 0:M], bank(7).rearrange("p (s m) -> p s m", m=M)).then_inc(s["s_copied"], 1)

            def exps(tile):
                act.wait_ge(s["p_dist"], LENT + tile + 1)
                act.activation(dist[:, :], dist[:, :], ACT.Exp).then_inc(s["e_done"], 1)

            def high_part(tile):
                act.wait_ge(s["t_full"], LENT + tile + 1)
                act.wait_ge(s["w_stored"], LENT + 48 * tile)
                act.copy(wp[:, 0, :, :].rearrange("p g n -> p (g n)"), bank(7)).then_inc(s["hi_done"], 1)
                act.wait_ge(s["b2_full"], LENT + tile)
                act.copy(wT[:, :, :].rearrange("p g n -> p (g n)"), bank(7)).then_inc(s["wT_done"], 1)

            def begin_sums(tile, blk, col):
                act.wait_ge(s["b2_full"], LENT + tile + 1)
                act.copy(ysum[:, ds(blk * 2 + 1, 2), ds(col, P)],
                         bank(7, 0, 2 * P).rearrange("p (a n) -> p a n", a=2)).then_inc(s["y_begun"], 1)

            act.wait_ge(s["ready"], 1)
            with act.Fori(0, LEAD) as i:
                copy_scores(i)
                exps(i)
                high_part(i)
                begin_sums(i, i // 4, (i % 4) * P)

            def iteration(i, prep):
                for n in range(8):
                    act.wait_ge(s["w2_done"], LENT + 8 * i + n)
                    for j in range(4):
                        u = 4 * n + j
                        act.wait_ge(s["a_full"], UNITS * i + u + 1)
                        act.activation(ring[:, u % 8, :], bank(u % 4), ACT.Gelu_apprx_tanh).then_inc(s["a_free"], 1)
                    if prep and n == 1:
                        copy_scores(i + LEAD)
                    if prep and n == 4:
                        exps(i + LEAD)
                    if prep and n == 6:
                        high_part(i + LEAD)
                    if prep and n == 7:
                        begin_sums(i + LEAD, (i + LEAD) // 4, ((i + LEAD) % 4) * P)

            act.wait_ge(s["ready"], 1)
            act.copy(act_carrier[:, :], ident[:, 0:1]).then_inc(s["a_free"], 4)
            with act.Fori(0, NIT - LEAD) as i:
                iteration(i, True)
            with act.Fori(NIT - LEAD, NIT) as i:
                iteration(i, False)
            with act.Fori(0, NBLK) as i:
                act.wait_ge(s["fin_u"], i + 1)
                act.wait_ge(s["fin_o"], LENT + i)
                act.activation(uT[0:GH, :], bank(0, 0, 512, 0, GH), ACT.Gelu_apprx_tanh,
                               bias=g1b[:, :]).then_inc(s["fin_g"], 1)

        @block.vector
        def _(dve):
            links = [0]

            def link(ins):
                links[0] += 1
                ins.then_inc(s["dchain"], 1)
                dve.wait_ge(s["dchain"], links[0])

            dve.memset(h[:, TILES:TILES + 2, :], 0.0)
            dve.memset(stats[:, TILES:TILES + 2, :], 0.0)
            link(dve.memset(pix[:, :, :], 1.0))
            dve.wait_ge(s["ld_img"], 16 * 7)
            dve.tensor_scalar(row_hot[:, :], curve_bc[:, :, 1], iota_p[0:IMG, 0:1], None, ALU.is_equal).then_inc(s["hot"], 1)
            link(dve.tensor_copy(curve_f[:, :, :], curve_n[:, :, :]))
            for n in range(2):
                ins = dve.tensor_scalar(col_hot[:, n, :], iota_x[:, :], curve_f[:, n, 0:1], None, ALU.is_equal)
            link(ins)
            dve.wait_ge(s["seen"], 1)
            for n in range(2):
                link(dve.tensor_tensor(picked.rearrange("p (k b x) -> p k b x", k=3, x=IMG),
                                       ps[:, 3 * n * 512:(3 * n + 3) * 512].rearrange("p (k f) -> p k f", k=3)[:, :, 0:384]
                                       .rearrange("p k (b x) -> p k b x", x=IMG),
                                       _mid2(col_hot[:, n, :], 3, 4), ALU.mult))
                ins = dve.tensor_reduce(pix[:, n, 0:B * CIN], picked.rearrange("p (n x) -> p n x", x=IMG), AXX, ALU.add)
                if n == 0:
                    link(ins)
            ins.then_inc(s["picked_s"], 1)

            def moments(n, extra):
                st = stats[:, :, :]
                link(dve.tensor_tensor(lns[:, 0, :], st[:, :, 1], st[:, :, 4], ALU.add))
                link(dve.tensor_scalar(mean[:, :], lns[:, 0, :], 0.5, None, ALU.mult))
                link(dve.tensor_tensor(lns[:, 1, :], st[:, :, 1], st[:, :, 4], ALU.subtract))
                link(dve.tensor_tensor(lns[:, 0, :], lns[:, 1, :], lns[:, 1, :], ALU.mult))
                link(dve.tensor_tensor(lns[:, 1, :], st[:, :, 2], st[:, :, 5], ALU.add))
                link(dve.tensor_scalar(lns[:, 1, :], lns[:, 1, :], 1.0 / D, EPS, ALU.mult, ALU.add))
                dve.scalar_tensor_tensor(lns[:, 2, :], lns[:, 0, :], 0.25, lns[:, 1, :], ALU.mult,
                                         ALU.add).then_inc(s["ln_var"], 1)
                dve.wait_ge(s["ln_std"], n)
                link(dve.reciprocal(rstd[:, :], lns[:, 3, :]))

            dve.wait_ge(s["image"], 1)
            dve.wait_ge(s["ld_text"], 64)
            with dve.Fori(0, TILES) as i:
                dve.bn_stats(stats[:, ds(i, 1), :].rearrange("p o k -> p (o k)"),
                             h[:, ds(i, 1), :].rearrange("p o e -> p (o e)")).then_inc(s["st1"], 1)
            dve.wait_ge(s["st1"], TILES)
            moments(1, 0)

            def xn_make(n):
                dve.wait_ge(s["xn_t"], LENT + n)
                for x in range(2):
                    ins = dve.tensor_scalar(xn[:, x, :], h[:, ds(n * 2 + x, 1), :].rearrange("p o e -> p (o e)"),
                                            mean[:, ds(n * 2 + x, 1)], rstd[:, ds(n * 2 + x, 1)],
                                            ALU.subtract, ALU.mult)
                ins.then_inc(s["xn_d"], 1)

            xn_make(0)
            dve.wait_ge(s["ld_attn"], 16 * 6)

            def table(c, n, a, b):
                v = rope[:, ds(c, 1), n, a:b].rearrange("p o d -> p (o d)")
                return _mid(v, H)

            def rotate(x, kind, k, c):
                what = "qk"[kind]
                to = 2 * kind
                src = ps[:, to * 512:to * 512 + QK].rearrange("p (h d) -> p h d", d=DQK)
                dve.wait_ge(s[f"{what}{x}"], k + 1)
                dve.wait_ge(s[f"a{what}{x}"], LENT + k)
                dve.wait_ge(s[f"o{x}"], LENT + k)
                n = 2 * x + kind
                hd = DQK // 2
                dve.tensor_tensor(t1[:, n, :, :], src, table(c, 2 * kind, 0, DQK), ALU.mult)
                dve.tensor_tensor(t2[:, n, :, 0:hd], src[:, :, hd:], table(c, 2 * kind + 1, 0, hd), ALU.mult)
                dve.tensor_tensor(t2[:, n, :, hd:], src[:, :, 0:hd], table(c, 2 * kind + 1, hd, DQK),
                                  ALU.mult).then_inc(s[f"r{what}{x}"], 1)

            def values(x, k, c):
                dve.wait_ge(s[f"v{x}"], k + 1)
                dve.tensor_tensor(vn[:, x, :, :], bank(4 + 2 * x, 0, HV).rearrange("p (h v) -> p h v", v=DV),
                                  _last(vscale[:, ds(c, 1), :].rearrange("p o h -> p (o h)"), DV),
                                  ALU.mult).then_inc(s[f"ve{x}"], 1)

            with dve.Fori(0, 2) as bb:
                dve.wait_ge(s["o0"], LENT + bb * CH)
                dve.wait_ge(s["o1"], LENT + bb * CH)
                dve.wait_ge(s["se1"], LENT + bb * CH)
                dve.memset(state[:, :, :, :], 0.0).then_inc(s["reset"], 1)
                with dve.Fori(0, CH) as c:
                    k = bb * CH + c
                    rotate(0, 0, k, c)
                    rotate(0, 1, k, c)
                    values(0, k, c)
                    rotate(1, 0, k, c)
                    rotate(1, 1, k, c)
                    values(1, k, c)
                    xn_make(k + 1)
                    for x in range(2):
                        dve.wait_ge(s[f"sc{x}"], k + 1)
                        to = 4 + 2 * x
                        dve.tensor_tensor(pT[:, x, :, :], ps[:, to * 512:to * 512 + QK].rearrange("p (h n) -> p h n", n=P),
                                          _mid(causal[:, :], H), ALU.mult).then_inc(s[f"m{x}"], 1)
                    dve.wait_ge(s["reset"], bb + 1)
                    for x in range(2):
                        dve.wait_ge(s[f"o{x}"], LENT + k + 1)
                        dve.tensor_tensor(oT[:, ds(k * 2 + x, 1), :, :].rearrange("p o g n -> p (o g n)"),
                                          bank(2 * x, 0, HV),
                                          oscale[:, ds(c, 1), :, :].rearrange("p o g n -> p (o g n)"),
                                          ALU.mult).then_inc(s[f"oe{x}"], 1)
                        dve.wait_ge(s[f"se{x}"], LENT + k)
                        sx = state[:, x, :, :].rearrange("p h v -> p (h v)")
                        dve.tensor_tensor(sx, bank(2 * x + 1, 0, HV), sx, ALU.add).then_inc(s[f"se{x}"], 1)
                    for x in range(2):
                        dve.wait_ge(s[f"oe{x}"], LENT + k + 1)
                        for g in range(VP):
                            ins = dve.bn_stats(gns[:, ds(k * 2 + x, 1), g, :].rearrange("p o k -> p (o k)"),
                                               oT[:, ds(k * 2 + x, 1), g, :].rearrange("p o n -> p (o n)"))
                    ins.then_inc(s["st1"], 1)
            dve.wait_ge(s["st1"], TILES + PAIRS)
            attention_over(dve)
            for b in range(B):
                first = 12 * (b // 2) + b % 2
                for g in range(VP):
                    ins = dve.bn_aggr(gmv[:, b, g, :], gns[:, first:first + 11:2, g, :])
            ins.then_inc(s["gn_in"], 1)
            dve.wait_ge(s["b_hi"], 1)
            dve.tensor_tensor(w1f[:, :], w1f[:, :], w1p[:, 0, :], ALU.subtract)
            dve.tensor_tensor(b1f[:, :], b1f[:, :], b1p[:, 0, :], ALU.subtract).then_inc(s["b_r"], 1)
            dve.wait_ge(s["gn_m"], 1)
            m1 = bank(0, 0, 24).rearrange("p (b g k) -> p b g k", b=B, g=VP)
            link(dve.tensor_tensor(gtmp[:, 0, :, :], gmv[:, :, :, 0], m1[:, :, :, 0], ALU.subtract))
            dve.tensor_tensor(gtmp[:, 1, :, :], gtmp[:, 0, :, :], gtmp[:, 0, :, :], ALU.mult).then_inc(s["gn_dev"], 1)
            link(dve.tensor_scalar(gtmp[:, 4, :, :], m1[:, :, :, 1], EPS, None, ALU.add))
            link(dve.tensor_copy(gtmp[:, 5, :, :], m1[:, :, :, 0]))
            dve.wait_ge(s["gn_v"], 1)
            dve.tensor_tensor(gtmp[:, 2, :, :], bank(1, 0, 12).rearrange("p (b g) -> p b g", b=B), gtmp[:, 4, :, :],
                              ALU.add).then_inc(s["gn_std"], 1)
            dve.wait_ge(s["b_mid"], 1)
            dve.tensor_tensor(w1p[:, 2, :], w1f[:, :], w1p[:, 1, :], ALU.subtract)
            dve.tensor_tensor(b1p[:, 2, :], b1f[:, :], b1p[:, 1, :], ALU.subtract).then_inc(s["z_lo"], 1)
            dve.wait_ge(s["gn_std"], 2)
            dve.wait_ge(s["ld_late"], 16 * 12)
            link(dve.reciprocal(gtmp[:, 0, :, :], gtmp[:, 3, :, :]))
            link(dve.tensor_tensor(gscale[:, :, :], gtmp[:, 0, :, :], _mid(gnw[:, :], B), ALU.mult))
            link(dve.tensor_tensor(gtmp[:, 4, :, :], gtmp[:, 5, :, :], gscale[:, :, :], ALU.mult))
            dve.tensor_tensor(gbias[:, :, :], _mid(gnb[:, :], B), gtmp[:, 4, :, :], ALU.subtract).then_inc(s["gn_done"], 1)
            with dve.Fori(0, PAIRS) as k:
                for x in range(2):
                    dve.wait_ge(s["yn"], k * 2 + x + 1)
                    v = yg[:, x, :, :].rearrange("p g n -> p (g n)")
                    dve.tensor_tensor(v, v, gate[:, ds(k * 2 + x, 1), :, :].rearrange("p o g n -> p (o g n)"),
                                      ALU.mult).then_inc(s["yg_d"], 1)
                for x in range(2):
                    hx = h[:, ds(k * 2 + x, 1), :].rearrange("p o e -> p (o e)")
                    dve.wait_ge(s["wo_s"], LENT + k * 2 + x + 1)
                    dve.tensor_tensor(hx, bank(2 + x, 0, D), hx, ALU.add).then_inc(s["res"], 1)
                    dve.wait_ge(s["res"], LENT + k * 2 + x + 1)
                    dve.bn_stats(stats[:, ds(k * 2 + x, 1), :].rearrange("p o k -> p (o k)"), hx).then_inc(s["st1"], 1)
            dve.wait_ge(s["st1"], TILES + PAIRS + TILES)
            dve.wait_ge(s["dchain"], links[0])
            moments(2, 0)
            dve.wait_ge(s["yg_d"], TILES)
            dve.memset(ring[:, :, :], 0.0)
            dve.memset(ysum[:, :, :], 0.0)
            dve.memset(zst[:, :, :, :], 0.0)
            dve.memset(wst[:, :, :, :], 0.0)
            dve.memset(w2cur[:, :, :, :], 0.0)
            dve.memset(uT[:, :], 1.0)
            link(dve.memset(norm[:, :, :], 0.0))
            link(dve.memset(zst[96:99, :, :, :], 1.0))
            dve.memset(sc[:, :, M:M + 4], FILLER).then_inc(s["z_r"], 1)
            with dve.Fori(0, NBLK) as i:
                dve.wait_ge(s["x2_t"], LENT + i)
                for n in range(4):
                    ins = dve.tensor_scalar(x2[:, n, :], h[:, ds(i * 4 + n, 1), :].rearrange("p o e -> p (o e)"),
                                            mean[:, ds(i * 4 + n, 1)], rstd[:, ds(i * 4 + n, 1)],
                                            ALU.subtract, ALU.mult)
                ins.then_inc(s["x2_d"], 1)
                dve.wait_ge(s["z_hi"], i + 1)
                dve.tensor_tensor(zr[:, :], bank(6), zp[:, 0, :], ALU.subtract).then_inc(s["z_r"], 1)
                dve.wait_ge(s["z_mid"], i + 1)
                dve.wait_ge(s["z_r"], i + 2)
                dve.tensor_tensor(zp[:, 2, :], zr[:, :], zp[:, 1, :], ALU.subtract).then_inc(s["z_lo"], 1)

            def place_z(tile):
                dve.wait_ge(s["s_full"], LENT + tile)
                dve.tensor_copy(zcur[:, :], zT[:, ds(tile * P, P)]).then_inc(s["zc"], 1)

            def carry_waits():
                dve.memset(carrier[:, :], 0.0)

            def search(tile):
                dve.wait_ge(s["s_copied"], tile + 1)
                dve.wait_ge(s["p_dist"], LENT + tile)
                dve.wait_ge(s["p_taken"], LENT + tile)
                carry_waits()
                for g in range(S):
                    ins = dve.max(top8[:, g, :], sc[:, g, 0:M])
                ins.then_inc(s["t_top"], 1)
                dve.wait_ge(s["t_top"], tile * 3 + 1)
                dve.tensor_copy(top4[:, :, :], top8[:, :, 0:TOPK]).then_inc(s["t_top"], 1)
                dve.wait_ge(s["t_top"], tile * 3 + 2)
                dve.memset(top8[:, :, TOPK:8], FILLER).then_inc(s["t_top"], 1)
                dve.wait_ge(s["t_top"], tile * 3 + 3)
                carry_waits()
                for g in range(S):
                    ins = dve.match_replace(mr[:, g, :], top8[:, g, :], sc[:, g, :], TAKEN)
                ins.then_inc(s["t_mr"], 1)

            def normaliser(tile):
                dve.wait_ge(s["e_done"], tile + 1)
                dve.wait_ge(s["p_w"], LENT + tile)
                dve.tensor_reduce(norm[:, 0, :], dist[:, S * M:].rearrange("p (s k) -> p s k", k=TOPK), AXX,
                                  ALU.add).then_inc(s["n_done"], 1)
                dve.wait_ge(s["n_done"], LENT + tile * 3 + 1)
                dve.tensor_scalar(norm[:, 0, :], norm[:, 0, :], -TAKEN, None, ALU.mult).then_inc(s["n_done"], 1)
                dve.wait_ge(s["n_done"], LENT + tile * 3 + 2)
                dve.reciprocal(norm[:, 1, :], norm[:, 0, :]).then_inc(s["n_done"], 1)

            def remainder(tile):
                dve.wait_ge(s["wT_done"], tile + 1)
                dve.wait_ge(s["lo_done"], LENT + tile)
                dve.tensor_tensor(wr[:, :, :].rearrange("p g n -> p (g n)"), bank(7),
                                  wp[:, 0, :, :].rearrange("p g n -> p (g n)"), ALU.subtract).then_inc(s["r_done"], 1)

            dve.wait_ge(s["z_r"], NBLK + 1)
            dve.memset(carrier[:, :], 0.0).then_inc(s["ready"], 1)
            dve.wait_ge(s["ready"], 1)
            with dve.Fori(0, LEAD) as i:
                place_z(i)
                search(i)
                normaliser(i)
                remainder(i)

            def keep_sums(i, slot, begun):
                dve.wait_ge(s["w2_done"], LENT + 8 * i + 1)
                dve.wait_ge(s["y_kept"], LENT + i)
                dve.wait_ge(s["y_begun"], LENT + begun)
                v = ysum[:, slot, :].rearrange("p o n -> p (o n)")
                dve.tensor_tensor(v, bank(6), v, ALU.add).then_inc(s["y_kept"], 1)

            def iteration(i, prep):
                for n in range(8):
                    for j in range(4):
                        u = 4 * n + j
                        dve.wait_ge(s["a_free"], UNITS * i + u + 1 + 4)
                        dve.wait_ge(s["w_full"], LENT + UNITS * i + u + 1)
                        dve.tensor_tensor(ring[:, u % 8, :], bank(4 + u % 2), ring[:, u % 8, :],
                                          ALU.mult).then_inc(s["w_free"], 1)
                    if n == 0:
                        if prep:
                            place_z(i + LEAD)
                        keep_sums(i, ds((i + 1) // 2, 1), i + LEAD - 1 if prep else TILES)
                    if prep and n == 2:
                        search(i + LEAD)
                    if prep and n == 5:
                        normaliser(i + LEAD)
                    if prep and n == 6:
                        remainder(i + LEAD)

            dve.memset(carrier[:, :], 0.0).then_inc(s["w_free"], 2)
            with dve.Fori(0, NIT - LEAD) as i:
                iteration(i, True)
            with dve.Fori(NIT - LEAD, NIT) as i:
                iteration(i, False)
            keep_sums(NIT, slice(12, 13), TILES)
            dve.wait_ge(s["y_kept"], LENT + NIT + 1)
            dve.memset(carrier[:, :], 0.0).then_inc(s["fin_y"], NBLK)
            with dve.Fori(0, NBLK) as i:
                dve.wait_ge(s["fin_o"], LENT + i + 1)
                v = h[:, ds(i * 4, 4), :]
                src = ps[:, 512:5 * 512].rearrange("p (n f) -> p n f", n=4)[:, :, 0:D]
                dve.tensor_tensor(v, src, v, ALU.add).then_inc(s["fin_h"], 1)

        @block.gpsimd
        def _(pool):
            for n in lent:
                pool.nop().then_inc(s[n], LENT)
            with pool.Fori(0, PAIRS) as k:
                for x in range(2):
                    for kind, what in enumerate("qk"):
                        n = 2 * x + kind
                        pool.wait_ge(s[f"r{what}{x}"], k + 1)
                        pool.tensor_tensor(t1[:, n, :, :].rearrange("p h d -> p (h d)"),
                                           t1[:, n, :, :].rearrange("p h d -> p (h d)"),
                                           t2[:, n, :, :].rearrange("p h d -> p (h d)"),
                                           ALU.add).then_inc(s[f"a{what}{x}"], 1)

            def gates(tile):
                pool.wait_ge(s["p_em"], LENT + tile)
                pool.wait_ge(s["n_done"], LENT + tile * 3)
                pool.wait_ge(s["t_top"], tile * 3 + 3)
                pool.wait_ge(s["s_copied"], tile + 1)
                pool.tensor_tensor(dist[:, 0:S * M].rearrange("p (s m) -> p s m", m=M), sc[:, :, 0:M],
                                   _last(top4[:, :, 0], M), ALU.subtract)
                pool.tensor_tensor(dist[:, S * M:].rearrange("p (s k) -> p s k", k=TOPK), top4[:, :, :],
                                   _last(top4[:, :, 0], TOPK), ALU.subtract).then_inc(s["p_dist"], 1)
                pool.wait_ge(s["t_mr"], LENT + tile + 1)
                pool.tensor_tensor(taken[:, :, :], sc[:, :, 0:M], mr[:, :, 0:M], ALU.subtract).then_inc(s["p_taken"], 1)
                pool.wait_ge(s["p_taken"], LENT + tile + 1)
                pool.wait_ge(s["e_done"], tile + 1)
                pool.wait_ge(s["t_full"], LENT + tile)
                pool.tensor_tensor(taken[:, :, :], dist[:, 0:S * M].rearrange("p (s m) -> p s m", m=M),
                                   taken[:, :, :], ALU.mult).then_inc(s["p_em"], 1)
                pool.wait_ge(s["p_em"], LENT + tile + 1)
                pool.wait_ge(s["n_done"], LENT + tile * 3 + 3)
                pool.tensor_tensor(wn[:, :, :], taken[:, :, :], _last(norm[:, 1, :], M), ALU.mult).then_inc(s["p_w"], 1)
                settle(pool)
                pool.wait_ge(s["r_done"], tile + 1)
                pool.tensor_copy(wp[:, 1, :, :], wr[:, :, :]).then_inc(s["mid_done"], 1)
                pool.wait_ge(s["mid_done"], tile + 1)
                pool.tensor_tensor(wp[:, 2, :, :], wr[:, :, :], wp[:, 1, :, :], ALU.subtract).then_inc(s["lo_done"], 1)

            pool.wait_ge(s["ready"], 1)
            with pool.Fori(0, TILES) as i:
                gates(i)


def _mid(v, n):
    return v.rearrange("p (o d) -> p o d", o=1).to_broadcast([v.shape[0], n, v.shape[1]])


def _mid2(v, n, m):
    return v.rearrange("p (o q d) -> p o q d", o=1, q=1).to_broadcast([v.shape[0], n, m, v.shape[1]])


def _last(v, n):
    return v.rearrange("p (d o) -> p d o", o=1).to_broadcast([v.shape[0], v.shape[1], n])


def _bcast(v, n):
    return v.rearrange("(o n) c -> o n c", o=1).to_broadcast([n, v.shape[0], v.shape[1]])


def _gate_rows(w_parts, k, a, kt, blk):
    v = w_parts[k, :, ds(blk * BLK, BLK)].rearrange("(a j e m) n -> a e m j n", a=2, j=4, e=2)
    return v[ds(a, 1), ds(kt, 1)].rearrange("a e m j n -> (a e m) j n")


def constants():
    import numpy as np

    pos = np.arange(T, dtype=np.float64)
    half = DQK // 2
    inv = 1.0 / 10000.0 ** (np.arange(half) / half)
    angle = (pos[:, None] * inv[None, :].astype(np.float32)).astype(np.float32).astype(np.float64)
    zeta = (np.arange(half) + half) / DQK
    grow = zeta[None, :] ** (pos[:, None] / 512.0)
    tabs = []
    for decay in (grow, 1.0 / grow):
        c, sn = np.cos(angle) * decay, np.sin(angle) * decay
        tabs += [np.concatenate([c, c], 1), np.concatenate([-sn, sn], 1)]
    rope = np.stack(tabs, 1).reshape(CH, P, 4, P).transpose(1, 0, 2, 3)
    gamma = 1.0 - 2.0 ** (-(5.0 + np.arange(H)))
    row = (1 - gamma[:, None] ** (pos[None, :] + 1)) / (1 - gamma[:, None])
    osc = gamma[:, None] ** pos[None, :] / np.sqrt(row) * DQK ** -0.5
    osc = np.repeat(osc.reshape(VP, 2, 1, T), DV, 2).reshape(VP, P, CH, P).transpose(1, 2, 0, 3)
    vsc = (gamma[None, :] ** -pos[:, None]).reshape(CH, P, H).transpose(1, 0, 2)
    sel = np.zeros((3, 32, 8, 4, HID))
    for m in range(32):
        sel[:, m, m // 4, m % 4, :] = 1
    halves = np.kron(np.eye(2), np.ones((DV, DV))) / DV
    f = np.float32
    return {"rope": rope.astype(f), "oscale": osc.astype(f), "vscale": vsc.astype(f),
            "causal": np.triu(np.ones((P, P))).astype(f), "ident": np.eye(P, dtype=f),
            "sel": sel.reshape(96, 2, BLK).astype(f), "halves": halves.astype(f),
            "iota_p": np.arange(P, dtype=f)[:, None], "iota_x": np.tile(np.arange(IMG, dtype=f), (P, 1))}


def layouts(i):
    import numpy as np

    g = {k: np.asarray(v) for k, v in i.items()}
    f = np.float32
    wblk = np.zeros((B * CIN + 1, B * D), f)
    for b in range(B):
        wblk[CIN * b:CIN * b + CIN, D * b:D * b + D] = g["L0_tok_proj_w"].T
        wblk[B * CIN, D * b:D * b + D] = g["L0_tok_proj_b"]
    cblk = np.zeros((S, R, S, M), f)
    for k in range(S):
        cblk[k, :, k, :] = g["L0_ffn_C"][k].T
    w2 = np.zeros((2, 2, 4, HID, 8, 4, 32), f)
    w2[..., 0:R] = g["L0_ffn_W2"].reshape(2, 4, 2, 8, 4, HID, R).transpose(0, 2, 4, 5, 3, 1, 6)
    b2 = np.zeros((2, M, 4, 4, 32), f)
    for k in range(S):
        b2[k % 2, :, k // 2, k % 4, 0:R] = g["L0_ffn_b2"][k]
    g1 = np.zeros((4, 32, 2, GH), f)
    g1[:, 0:R] = g["L0_ffn_G1"].reshape(2, 4, R, GH).transpose(1, 2, 0, 3)
    return {
        "x": g["x"], "txt": g["txt"], "curve": g["L0_tok_curve"], "wblk": wblk,
        "wcat": np.concatenate([g["L0_attn_Wq"], g["L0_attn_Wk"], g["L0_attn_Wv"], g["L0_attn_Wg"]], 1),
        "wo": g["L0_attn_Wo"], "gnw": g["L0_attn_gn_weight"].reshape(VP, P).T,
        "gnb": g["L0_attn_gn_bias"].reshape(VP, P).T,
        "pw": g["L0_ffn_P"].transpose(1, 0, 2).reshape(D, S * R), "cblk": cblk.reshape(P, S * M),
        "w1": g["L0_ffn_W1"].transpose(0, 2, 1, 3).reshape(P, M * HID), "b1": g["L0_ffn_b1"].reshape(P, P),
        "w2": w2.reshape(4, P, 1024), "b2": b2.reshape(P, 4, P), "g1": g1.reshape(P, 2, GH),
        "g1b": g["L0_ffn_g1b"].reshape(GH, 1), "g2": np.concatenate([g["L0_ffn_G2"], g["L0_ffn_g2b"][None]], 0),
    }


def kernel(**inputs):
    import concourse.bacc as bacc
    import numpy as np
    from concourse.bass_utils import run_bass_kernel_spmd

    nc = bacc.Bacc("TRN2", target_bir_lowering=False, num_devices=1)
    arrays, aps = {}, {}
    for name, a in {**layouts(inputs), **constants()}.items():
        a = np.ascontiguousarray(a)
        arrays[f"in_{name}"] = a
        aps[name] = nc.dram_tensor(f"in_{name}", a.shape, mybir.dt.from_np(a.dtype), kind="ExternalInput").ap()
    aps["out"] = nc.dram_tensor("out_h", (B, T, D), F32, kind="ExternalOutput").ap()
    fused_layer(nc, aps)
    r = run_bass_kernel_spmd(nc, [arrays], core_ids=[0])
    return r.results[0]["out_h"]
```

```python
from contextlib import ExitStack

import concourse.bass as bass
from concourse import mybir

F32 = mybir.dt.float32
BF16 = mybir.dt.bfloat16
I32 = mybir.dt.int32
ALU = mybir.AluOpType
ACT = mybir.ActivationFunctionType
AXX = mybir.AxisListType.X

P = 128
B, CIN, IMG = 4, 3, 96
NPATCH, TXT, D = 256, 512, 192
D2 = D - P
T = NPATCH + TXT
CH = T // P
TILES = B * CH
PAIRS = TILES // 2
H, DQK, DV = 6, 128, 64
QK = H * DQK
HV = H * DV
VP = HV // P
S, R, M, TOPK, HID, GH = 8, 16, 64, 4, 32, 64
BLK = 512
NBLK = B * T // BLK
NIT = NBLK * 4
LEAD = 5
LENT = 1
UNITS = 32
RING = 16
AHEAD = 6
ABANK, WBANK, TURNS = 0, 3, 3
TAKEN = -2.0 ** 100
FILLER = -2.0 ** 101
EPS = 1e-5


def ds(start, size):
    return bass.ds(start, size)


def fused_layer(nc, t):
    out = t["out"]
    w1_parts = nc.dram_tensor("w1_parts", (3, P, M * HID), BF16, kind="Internal").ap()
    b1_parts = nc.dram_tensor("b1_parts", (3, P, P), BF16, kind="Internal").ap()
    z_parts = nc.dram_tensor("z_parts", (3, P, B * T), BF16, kind="Internal").ap()
    w_parts = nc.dram_tensor("w_parts", (3, S * M, B * T), BF16, kind="Internal").ap()

    with ExitStack() as ctx:
        def alloc(stack, name, shape, dt=F32):
            return stack.enter_context(nc.sbuf_tensor(name, shape, dt))

        def sb(name, shape, dt=F32):
            return alloc(ctx, name, shape, dt)

        def sem(name):
            return ctx.enter_context(nc.semaphore(name))

        h = sb("h", [P, TILES + 2, D])
        ident = sb("ident", [P, P])
        act_carrier = sb("act_carrier", [P, 1])
        halves = sb("halves", [P, P])
        stats = sb("stats", [P, TILES + 2, 6])
        mean = sb("mean", [P, TILES + 2])
        rstd = sb("rstd", [P, TILES + 2])
        gns = sb("gns", [P, TILES, VP, 6])
        lns = sb("lns", [P, 4, TILES + 2])

        with ExitStack() as region:
            oT = alloc(region, "oT", [P, TILES, VP, P])
            gate = alloc(region, "gate", [P, TILES, VP, P])
        with ExitStack() as region:
            ysum = alloc(region, "ysum", [P, 13, BLK])
            zst = alloc(region, "zst", [P, 2, 4, BLK], BF16)
            wst = alloc(region, "wst", [P, 2, 4, BLK], BF16)
            sc = alloc(region, "sc", [P, S, M + 4])
            mr = alloc(region, "mr", [P, S, M + 4])
            dist = alloc(region, "dist", [P, S * M + S * TOPK])
            taken = alloc(region, "taken", [P, S, M])
            wn = alloc(region, "wn", [P, S, M])
        gap = ctx.enter_context(nc.sbuf_tensor("region_one", [P, 2 * TILES * VP * P], F32))

        with ExitStack() as region:
            wcat = alloc(region, "wcat", [P, 2, 2 * QK + 2 * HV])
            rope = alloc(region, "rope", [P, CH, 4, P])
            oscale = alloc(region, "oscale", [P, CH, VP, P])
            vscale = alloc(region, "vscale", [P, CH, H])
            causal = alloc(region, "causal", [P, P])
            t1 = alloc(region, "t1", [P, 4, H, DQK])
            t2 = alloc(region, "t2", [P, 4, H, DQK])
            qkT = alloc(region, "qkT", [P, 4, H, P])
            pT = alloc(region, "pT", [P, 2, H, P])
            vn = alloc(region, "vn", [P, 2, H, DV])
            state = alloc(region, "state", [P, 2, H, DV])
            xn = alloc(region, "xn", [P, 2, D])
            xnT = alloc(region, "xnT", [P, 2, 2, P])
            xim = t1[0:IMG, 0:2, :, :].rearrange("p a h d -> p (a h d)")[:, 0:B * CIN * IMG]
            picked = pT[:, :, :, :].rearrange("p a h d -> p (a h d)")[:, 0:B * CIN * IMG]
            w1f = t2[:, :, :, :].rearrange("p a h d -> p (a h d)")[:, 0:M * HID]
            w1p = qkT[:, :, :, :].rearrange("p a h d -> p (a h d)").bitcast(BF16).rearrange("p (k n) -> p k n", k=3)
            b1f = vn[:, 0, 0:2, :].rearrange("p a h -> p (a h)")
            b1p = vn[:, 1, :, :].rearrange("p a h -> p (a h)").bitcast(BF16)[:, 0:3 * P].rearrange("p (k n) -> p k n", k=3)
            curve_bc = alloc(region, "curve_bc", [IMG, NPATCH, 2], I32)
            curve_n = alloc(region, "curve_n", [P, 2, 2], I32)
            curve_f = alloc(region, "curve_f", [P, 2, 2])
            iota_p = alloc(region, "iota_p", [P, 1])
            iota_x = alloc(region, "iota_x", [P, IMG])
            row_hot = alloc(region, "row_hot", [IMG, NPATCH])
            col_hot = alloc(region, "col_hot", [P, 2, IMG])
            pix = alloc(region, "pix", [P, 2, B * CIN + 1])
            pixT = alloc(region, "pixT", [B * CIN + 1, 2, P])
            wblk = alloc(region, "wblk", [B * CIN + 1, B * D])
        w1st = sb("w1st", [P, S, M * HID], BF16)
        zT = sb("zT", [P, B * T])
        w2cur = sb("w2cur", [P, 8, 4, 32])
        b2w = sb("b2w", [P, 4, P])
        sel = sb("sel", [96, 8, P], BF16)
        cblk = sb("cblk", [P, S * M])
        pw = sb("pw", [P, 2, P])
        g1 = sb("g1", [P, 2, GH])
        g1b = sb("g1b", [GH, 1])
        g2 = sb("g2", [GH + 1, D])
        uT = sb("uT", [GH + 1, BLK])
        wo = sb("wo", [P, VP, D])
        gnw = sb("gnw", [P, VP])
        gnb = sb("gnb", [P, VP])
        gmv = sb("gmv", [P, B, VP, 2])
        gtmp = sb("gtmp", [P, 6, B, VP])
        gscale = sb("gscale", [P, B, VP])
        gbias = sb("gbias", [P, B, VP])
        yg = sb("yg", [P, 4, VP, P])
        zcur = sb("zcur", [P, P])
        carrier = sb("carrier", [P, 1])
        top8 = sb("top8", [P, S, 8])
        top4 = sb("top4", [P, S, TOPK])
        norm = sb("norm", [P, 2, S])
        wp = sb("wp", [P, 3, 4, P], BF16)
        wr = sb("wr", [P, 4, P])
        wT = sb("wT", [P, 4, P])
        with ExitStack() as region:
            zp = alloc(region, "zp", [P, 3, BLK], BF16)
            zr = alloc(region, "zr", [P, BLK])
            x2 = alloc(region, "x2", [P, 4, D])
            x2T = alloc(region, "x2T", [P, 2, BLK])
        ring = sb("ring", [P, RING, BLK])
        del gap

        ps = ctx.enter_context(nc.psum_tensor("ps", [P, 8 * 512], F32))

        def bank(n, a=0, b=512, p0=0, p1=P):
            return ps[p0:p1, n * 512 + a:n * 512 + b]

        block = ctx.enter_context(nc.Block())
        names = ("ld_img ld_text ld_attn ld_late ld_w1 ld_scr st_w1 st_z hot seen picked_s pix_t pixt_s img image "
                 "st1 ln_var ln_std xn_d xn_t xn_e "
                 "q0 q1 k0 k1 v0 v1 g0 g1s rq0 rq1 rk0 rk1 ve0 ve1 ge0 ge1 aq0 aq1 ak0 ak1 tq0 tq1 tk0 tk1 "
                 "eq0 eq1 ek0 ek1 sc0 sc1 m0 m1 st0s st1s o0 o1 oe0 oe1 se0 se1 reset dchain "
                 "gn_in gn_m gn_dev gn_v gn_std gn_done yn yg_d wo_s res "
                 "x2_d x2_t x2_e z_s z_hi z_r z_mid z_lo b_hi b_r b_mid "
                 "a_full a_free w_full w_free w2_done y_kept zc s_full s_copied t_top t_mr p_dist p_taken e_done "
                 "n_done p_em p_w t_full hi_done r_done mid_done lo_done w_stored stack w2_lo w2_hi wT_done b2_full y_begun sel_cast "
                 "ready cleared w1_lo fin_y fin_u fin_g fin_o fin_h stored").split()
        s = {n: sem(n) for n in names}
        lent = ("oe0 se0 oe1 se1 m0 m1 o0 o1 aq0 aq1 ak0 ak1 x2_e x2_t z_s res wo_s y_begun "
                "t_mr p_dist p_taken b2_full w_stored st_z fin_o fin_h s_full p_w lo_done t_full p_em n_done w2_done y_kept w_full xn_t z_r z_lo").split()

        def attention_over(eng):
            for n in ("oe0", "oe1", "se0", "se1", "ge0", "ge1", "xn_e"):
                eng.wait_ge(s[n], PAIRS + (n == "xn_e") + LENT * (n in lent))

        def settle(eng):
            eng.wait_ge(s["ready"], 1)

        @block.sync
        def _(sp):
            sp.dma_start(curve_bc[:, :, :], _bcast(t["curve"], IMG)).then_inc(s["ld_img"], 16)
            sp.dma_start(curve_n[:, :, :], t["curve"].rearrange("(n p) c -> p n c", p=P)).then_inc(s["ld_img"], 16)
            sp.dma_start(iota_p[:, :], t["iota_p"]).then_inc(s["ld_img"], 16)
            sp.dma_start(iota_x[:, :], t["iota_x"]).then_inc(s["ld_img"], 16)
            sp.dma_start(xim.rearrange("p (n x) -> p n x", x=IMG),
                         t["x"].rearrange("b c y x -> y (b c) x")).then_inc(s["ld_img"], 16)
            sp.dma_start(wblk[:, :], t["wblk"]).then_inc(s["ld_img"], 16)
            sp.dma_start(ident[:, :], t["ident"]).then_inc(s["ld_img"], 16)
            for b in range(B):
                first = 12 * (b // 2) + 4 + b % 2
                sp.dma_start(h[:, first:first + 7:2, :],
                             t["txt"][b].rearrange("(c p) e -> p c e", p=P)).then_inc(s["ld_text"], 16)
            sp.dma_start(w1f, t["w1"]).then_inc(s["ld_w1"], 16)
            sp.dma_start(b1f, t["b1"]).then_inc(s["ld_w1"], 16)
            sp.dma_start(wcat[:, 0, :], t["wcat"][0:P, :]).then_inc(s["ld_attn"], 16)
            sp.dma_start(wcat[0:D2, 1, :], t["wcat"][P:D, :]).then_inc(s["ld_attn"], 16)
            sp.dma_start(rope[:, :, :, :], t["rope"]).then_inc(s["ld_attn"], 16)
            sp.dma_start(oscale[:, :, :, :], t["oscale"]).then_inc(s["ld_attn"], 16)
            sp.dma_start(vscale[:, :, :], t["vscale"]).then_inc(s["ld_attn"], 16)
            sp.dma_start(causal[:, :], t["causal"]).then_inc(s["ld_attn"], 16)
            sp.dma_start(halves[:, :], t["halves"]).then_inc(s["ld_attn"], 16)
            sp.wait_ge(s["w1_lo"], 1)
            for k in range(3):
                sp.dma_start(w1_parts[k], w1p[:, k, :]).then_inc(s["st_w1"], 16)
                sp.dma_start(b1_parts[k], b1p[:, k, :]).then_inc(s["st_w1"], 16)
            attention_over(sp)
            for dst, src in ((gnw[:, :], t["gnw"]), (gnb[:, :], t["gnb"]),
                             (wo[:, :, :], t["wo"].rearrange("(c p) e -> p c e", p=P)),
                             (pw[:, 0, :], t["pw"][0:P, :]), (pw[0:D2, 1, :], t["pw"][P:D, :]),
                             (cblk[:, :], t["cblk"]), (b2w[:, :, :], t["b2"]), (x2T[0:96, :, :], t["sel"]),
                             (g1[:, :, :], t["g1"]), (g1b[:, :], t["g1b"]), (g2[:, :], t["g2"])):
                sp.dma_start(dst, src).then_inc(s["ld_late"], 16)
            sp.wait_ge(s["st_w1"], 96)
            for n, k in enumerate((0, 1, 0, 2, 0, 1)):
                sp.dma_start(w1st[R * n:R * n + R, :, :],
                             w1_parts[k].rearrange("(s r) n -> r s n", r=R)).then_inc(s["ld_scr"], 16)
            for k in range(3):
                sp.dma_start(w1st[96 + k:97 + k, :, :],
                             b1_parts[k].rearrange("(o s a) n -> o s (a n)", o=1, s=S)).then_inc(s["ld_scr"], 16)

            def store_z(i):
                sp.wait_ge(s["z_lo"], LENT + i + 1)
                sp.dma_start(z_parts[:, :, ds(i * BLK, BLK)].rearrange("k p n -> p k n"),
                             zp[:, :, :]).then_inc(s["st_z"], 16)

            def store_gates(tile):
                sp.wait_ge(s["lo_done"], LENT + tile + 1)
                for k in range(3):
                    sp.dma_start(w_parts[k, :, ds(tile * P, P)].rearrange("(g p) n -> p g n", p=P),
                                 wp[:, k, :, :]).then_inc(s["w_stored"], 16)

            def load_stack(i, par, blk, a, kt):
                for n, k in enumerate((0, 0, 1, 0, 2, 1)):
                    sp.dma_start(zst[R * n:R * n + R, ds(par, 1), :, :].rearrange("p o j n -> p (o j) n"),
                                 z_parts[k, ds(a * (4 * R), 4 * R), ds(blk * BLK, BLK)]
                                 .rearrange("(j r) n -> r j n", r=R)).then_inc(s["stack"], 16)
                for k in range(3):
                    sp.dma_start(wst[32 * k:32 * k + 32, ds(par, 1), :, :].rearrange("p o j n -> p (o j) n"),
                                 _gate_rows(w_parts, k, a, kt, blk)).then_inc(s["stack"], 16)

            def load_w2(i, combo, half):
                sp.dma_start(w2cur[:, 4 * half:4 * half + 4, :, :].rearrange("p q j r -> p (q j r)"),
                             t["w2"][ds(combo, 1), :, 512 * half:512 * half + 512]
                             .rearrange("o p n -> (o p) n")).then_inc(s["w2_hi" if half else "w2_lo"], 16)

            store_z(0)
            with sp.Fori(0, LEAD) as i:
                store_z(i + 1)
                store_gates(i)
            sp.wait_ge(s["st_z"], LENT + 16 * NBLK)
            sp.wait_ge(s["w_stored"], LENT + 48 * LEAD)
            sp.wait_ge(s["cleared"], 1)
            load_stack(0, 0, 0, 0, 0)
            load_w2(0, 0, 0)

            def step(i, gates, last=False):
                sp.wait_ge(s["w2_done"], LENT + 8 * i + 1)
                load_w2(i, i % 4, 1)
                if last:
                    return
                sp.wait_ge(s["w_full"], LENT + UNITS * i)
                sp.wait_ge(s["stack"], 144 * (i + 1))
                sp.wait_ge(s["w_stored"], LENT + gates)
                n = i + 1
                load_stack(n, n % 2, n // 4, (n // 2) % 2, n % 2)
                sp.wait_ge(s["w2_done"], LENT + 8 * i + 5)
                load_w2(n, n % 4, 0)

            with sp.Fori(0, NIT - LEAD) as i:
                step(i, 48 * (i + LEAD))
                store_gates(i + LEAD)
            with sp.Fori(NIT - LEAD, NIT - 1) as i:
                step(i, 48 * TILES)
            step(NIT - 1, 48 * TILES, last=True)
            with sp.Fori(0, 2) as bb:
                with sp.Fori(0, 3) as cb:
                    blk = bb * 3 + cb
                    sp.wait_ge(s["fin_h"], LENT + blk + 1)
                    for x in range(2):
                        sp.dma_start(out[ds(bb * 2 + x, 1), ds(cb * 2 * P, 2 * P), :]
                                     .rearrange("o (k p) e -> p (o k) e", p=P),
                                     h[:, ds(blk * 4 + x, 3), :][:, 0:3:2, :]).then_inc(s["stored"], 16)
            sp.wait_ge(s["stored"], 16 * 2 * NBLK)

        @block.tensor
        def _(pe):
            pe.wait_ge(s["ld_img"], 16 * 7)
            pe.wait_ge(s["hot"], 1)
            for n in range(2):
                for k in range(3):
                    mm = pe.matmul(bank(3 * n + k, 0, 384), row_hot[:, n * P:n * P + P],
                                   xim[:, 384 * k:384 * k + 384], start=True, stop=True)
            mm.then_inc(s["seen"], 1)
            pe.wait_ge(s["picked_s"], 1)
            for n in range(2):
                mm = pe.transpose(bank(6, n * P, n * P + P, 0, B * CIN + 1), pix[:, n, :], ident[:, :])
            mm.then_inc(s["pix_t"], 1)
            pe.wait_ge(s["pixt_s"], 1)
            for n in range(2):
                for k in range(2):
                    mm = pe.matmul(bank(2 * n + k, 0, 384), pixT[:, n, :], wblk[:, 384 * k:384 * k + 384],
                                   start=True, stop=True)
            mm.then_inc(s["img"], 1)

            def xn_turn(n):
                pe.wait_ge(s["xn_d"], n + 1)
                for x in range(2):
                    pe.transpose(bank(4, x * P, x * P + P), xn[:, x, 0:P], ident[:, :])
                    mm = pe.transpose(bank(4, (2 + x) * P, (3 + x) * P, 0, D2), xn[:, x, P:D], ident[:, :])
                mm.then_inc(s["xn_t"], 1)

            pe.wait_ge(s["image"], 1)
            xn_turn(0)
            pe.wait_ge(s["ld_attn"], 16 * 7)

            def wide(to, x, col, n, name):
                for a in range(0, n, 512):
                    w = min(512, n - a)
                    pe.matmul(bank(to + a // 512, 0, w), xnT[:, x, 0, :], wcat[:, 0, col + a:col + a + w],
                              start=True, stop=False)
                    mm = pe.matmul(bank(to + a // 512, 0, w), xnT[0:D2, x, 1, :], wcat[0:D2, 1, col + a:col + a + w],
                                   start=False, stop=True)
                mm.then_inc(s[name], 1)

            def values_gates(to, x):
                wide(to, x, 2 * QK, HV, f"v{x}")
                for g in range(VP):
                    col = 2 * QK + HV + g * P
                    pe.matmul(bank(to + 1, g * P, g * P + P), wcat[:, 0, col:col + P], xnT[:, x, 0, :],
                              start=True, stop=False)
                    mm = pe.matmul(bank(to + 1, g * P, g * P + P), wcat[0:D2, 1, col:col + P], xnT[0:D2, x, 1, :],
                                   start=False, stop=True)
                mm.then_inc(s["g0" if x == 0 else "g1s"], 1)

            def turn(to, src, name):
                for e in range(H):
                    mm = pe.transpose(ps[:, to * 512 + e * P:to * 512 + e * P + P], src[:, e, :], ident[:, :])
                mm.then_inc(s[name], 1)

            def heads(x, k, to_s):
                for e in range(H):
                    mm = pe.matmul(ps[:, to_s * 512 + e * P:to_s * 512 + e * P + P], qkT[:, 2 * x + 1, e, :],
                                   qkT[:, 2 * x, e, :], start=True, stop=True)
                mm.then_inc(s[f"sc{x}"], 1)

            def outputs(x, to):
                for e in range(H):
                    mm = pe.matmul(bank(to + 1, e * DV, e * DV + DV), t1[:, 2 * x + 1, e, :], vn[:, x, e, :],
                                   start=True, stop=True)
                mm.then_inc(s[f"st{x}s"], 1)
                for g in range(VP):
                    for part in range(2):
                        for e in range(2):
                            o = bank(to, g * P, g * P + P, e * DV, e * DV + DV)
                            if part == 0:
                                mm = pe.matmul(o, vn[:, x, 2 * g + e, :], pT[:, x, 2 * g + e, :], start=True, stop=False)
                            else:
                                mm = pe.matmul(o, state[:, x, 2 * g + e, :], qkT[:, 2 * x, 2 * g + e, :],
                                               start=False, stop=True)
                mm.then_inc(s[f"o{x}"], 1)

            with pe.Fori(0, 2) as bb:
                with pe.Fori(0, CH) as c:
                    k = bb * CH + c
                    pe.wait_ge(s["xn_e"], k + 1)
                    pe.wait_ge(s["oe0"], LENT + k)
                    pe.wait_ge(s["se0"], LENT + k)
                    wide(0, 0, 0, QK, "q0")
                    pe.wait_ge(s["oe1"], LENT + k)
                    pe.wait_ge(s["se1"], LENT + k)
                    wide(2, 0, QK, QK, "k0")
                    pe.wait_ge(s["m0"], LENT + k)
                    values_gates(4, 0)
                    pe.wait_ge(s["rq0"], k + 1)
                    wide(0, 1, 0, QK, "q1")
                    pe.wait_ge(s["rk0"], k + 1)
                    wide(2, 1, QK, QK, "k1")
                    pe.wait_ge(s["m1"], LENT + k)
                    values_gates(6, 1)
                    pe.wait_ge(s["ve0"], k + 1)
                    xn_turn(k + 1)
                    pe.wait_ge(s["ve1"], k + 1)
                    pe.wait_ge(s["ge1"], k + 1)
                    pe.wait_ge(s["ak0"], LENT + k + 1)
                    turn(6, t1[:, 1], "tk0")
                    pe.wait_ge(s["aq1"], LENT + k + 1)
                    turn(0, t1[:, 2], "tq1")
                    pe.wait_ge(s["xn_e"], k + 2)
                    pe.wait_ge(s["ge0"], k + 1)
                    pe.wait_ge(s["aq0"], LENT + k + 1)
                    turn(4, t1[:, 0], "tq0")
                    pe.wait_ge(s["ak1"], LENT + k + 1)
                    turn(2, t1[:, 3], "tk1")
                    pe.wait_ge(s["eq0"], k + 1)
                    pe.wait_ge(s["ek0"], k + 1)
                    heads(0, k, 4)
                    pe.wait_ge(s["eq1"], k + 1)
                    pe.wait_ge(s["ek1"], k + 1)
                    heads(1, k, 6)
                    pe.wait_ge(s["reset"], bb + 1)
                    pe.wait_ge(s["m0"], LENT + k + 1)
                    outputs(0, 0)
                    pe.wait_ge(s["m1"], LENT + k + 1)
                    outputs(1, 2)

            pe.wait_ge(s["gn_in"], 1)
            pe.matmul(bank(0, 0, 24), halves[:, :], gmv[:, :, :, :].rearrange("p b g k -> p (b g k)"),
                      start=True, stop=True).then_inc(s["gn_m"], 1)
            pe.wait_ge(s["gn_dev"], 1)
            pe.matmul(bank(1, 0, 12), halves[:, :], gtmp[:, 1, :, :].rearrange("p b g -> p (b g)"),
                      start=True, stop=True).then_inc(s["gn_v"], 1)
            pe.wait_ge(s["ld_late"], 16 * 11)
            with pe.Fori(0, NBLK) as k:
                for x in range(4):
                    pe.wait_ge(s["yg_d"], k * 4 + x + 1)
                    pe.wait_ge(s["res"], LENT + k * 4)
                    for g in range(VP):
                        mm = pe.matmul(bank(2 + x, 0, D), yg[:, x, g, :], wo[:, g, :], start=(g == 0), stop=(g == VP - 1))
                    mm.then_inc(s["wo_s"], 1)

            def turn_x2(i):
                pe.wait_ge(s["x2_d"], i + 1)
                pe.wait_ge(s["x2_e"], LENT + i)
                for n in range(4):
                    pe.transpose(bank(4, n * P, n * P + P), x2[:, n, 0:P], ident[:, :])
                    mm = pe.transpose(bank(5, n * P, n * P + P, 0, D2), x2[:, n, P:D], ident[:, :])
                mm.then_inc(s["x2_t"], 1)

            def project_z(i):
                pe.wait_ge(s["x2_e"], LENT + i + 1)
                pe.wait_ge(s["z_r"], LENT + i)
                pe.matmul(bank(6), pw[:, 0, :], x2T[:, 0, :], start=True, stop=False)
                pe.matmul(bank(6), pw[0:D2, 1, :], x2T[0:D2, 1, :], start=False, stop=True).then_inc(s["z_s"], 1)

            def scores(tile):
                pe.wait_ge(s["y_begun"], LENT + tile)
                pe.wait_ge(s["zc"], tile + 1)
                pe.matmul(bank(7), zcur[:, :], cblk[:, :], start=True, stop=True).then_inc(s["s_full"], 1)

            def turn_gates(tile):
                pe.wait_ge(s["p_w"], LENT + tile + 1)
                for g in range(4):
                    mm = pe.transpose(bank(7, g * P, g * P + P),
                                      wn[:, 2 * g:2 * g + 2, :].rearrange("p s m -> p (s m)"), ident[:, :])
                mm.then_inc(s["t_full"], 1)

            def gated_b2(tile):
                pe.wait_ge(s["wT_done"], tile + 1)
                for a in range(2):
                    for g in range(2):
                        mm = pe.matmul(bank(7, a * P, a * P + P), b2w[:, 2 * a + g, :], wT[:, 2 * a + g, :],
                                       start=(g == 0), stop=(g == 1))
                mm.then_inc(s["b2_full"], 1)

            turn_x2(0)
            project_z(0)
            with pe.Fori(0, LEAD) as i:
                scores(i)
                turn_x2(i + 1)
                project_z(i + 1)
                turn_gates(i)
                gated_b2(i)

            pe.wait_ge(s["cleared"], 1)
            pe.wait_ge(s["z_r"], LENT + NBLK)
            pe.wait_ge(s["sel_cast"], 1)
            pe.matmul(bank(6), ring[:, RING - 1, 0:P], ring[:, RING - 1, :], start=True, stop=True)
            pe.wait_ge(s["ld_scr"], 16 * 9)

            w1flat = w1st[:, :, :].rearrange("p s n -> p (s n)")
            zflat = zst[:, :, :, :].rearrange("p a j n -> p (a j n)")
            wflat = wst[:, :, :, :].rearrange("p a j n -> p (a j n)")

            def turn_short(v):
                return 1 if v < UNITS % TURNS else 0

            def first(i, u):
                m = i + 1 if u >= UNITS else i
                v = u % UNITS
                n, j = v // 4, v % 4
                if v == 0:
                    pe.wait_ge(s["stack"], 144 * (m + 1))
                pe.wait_ge(s["a_free"], UNITS * i + u + 1 + turn_short(v))
                base = ((m // 2) % 2) * (4 * M * HID) + (m % 2) * (32 * HID)
                pe.matmul(bank(ABANK + v % TURNS), w1flat[0:99, ds(base + (j * (M * HID) + n * P), P)],
                          zflat[0:99, ds((m % 2) * (4 * BLK) + j * BLK, BLK)],
                          start=True, stop=True).then_inc(s["a_full"], 1)

            def second(n, wait):
                pe.wait_ge(s["w_free"], wait + TURNS)
                for j in range(4):
                    mm = pe.matmul(bank(6, 0, 512, 32 * j, 32 * j + 32), w2cur[:, n, j, :], ring[:, (4 * n + j) % RING, :],
                                   start=(n == 0), stop=(n == 7), skip_group_check=True)
                mm.then_inc(s["w2_done"], 1)
                return mm

            def iteration(i, prep, last=False):
                for n in range(8):
                    for j in range(4):
                        u = 4 * n + j
                        pe.wait_ge(s["w_free"], UNITS * i + u + 1 + turn_short(u))
                        pe.matmul(bank(WBANK + u % TURNS), sel[:, n, :],
                                  wflat[0:96, ds((i % 2) * (4 * BLK) + j * BLK, BLK)],
                                  start=True, stop=True).then_inc(s["w_full"], 1)
                        if not last or u + AHEAD < UNITS:
                            first(i, u + AHEAD)
                    if n == 0:
                        second(7, UNITS * i)
                    else:
                        if n == 1:
                            pe.wait_ge(s["y_kept"], LENT + i + 1)
                            pe.wait_ge(s["w2_lo"], 16 * (i + 1))
                        if n == 5:
                            pe.wait_ge(s["w2_hi"], 16 * (i + 1))
                        second(n - 1, UNITS * i + 4 * n)
                    if prep and n == 0:
                        scores(i + LEAD)
                    if prep and n == 5:
                        turn_gates(i + LEAD)
                    if prep and n == 6:
                        gated_b2(i + LEAD)

            for u in range(AHEAD):
                first(0, u)
            with pe.Fori(0, NIT - LEAD) as i:
                iteration(i, True)
            with pe.Fori(NIT - LEAD, NIT - 1) as i:
                iteration(i, False)
            iteration(NIT - 1, False, last=True)
            second(7, UNITS * NIT)
            with pe.Fori(0, NBLK) as i:
                pe.wait_ge(s["fin_y"], i + 1)
                for a in range(2):
                    mm = pe.matmul(bank(0, 0, 512, 0, GH), g1[:, a, :], ysum[:, ds(i * 2 + a + 1, 1), :]
                                   .rearrange("p o n -> p (o n)"), start=(a == 0), stop=(a == 1))
                mm.then_inc(s["fin_u"], 1)
                pe.wait_ge(s["fin_g"], i + 1)
                pe.wait_ge(s["fin_h"], LENT + i)
                for n in range(4):
                    mm = pe.matmul(bank(1 + n, 0, D), uT[:, n * P:n * P + P], g2[:, :], start=True, stop=True)
                mm.then_inc(s["fin_o"], 1)

        @block.scalar
        def _(act):
            act.wait_ge(s["ld_w1"], 32)
            act.copy(w1p[:, 0, :], w1f)
            act.copy(b1p[:, 0, :], b1f).then_inc(s["b_hi"], 1)
            act.wait_ge(s["pix_t"], 1)
            act.copy(pixT[:, :, :], bank(6, 0, 2 * P, 0, B * CIN + 1).rearrange("p (n t) -> p n t", n=2)).then_inc(s["pixt_s"], 1)
            act.wait_ge(s["img"], 1)
            for n in range(2):
                for k in range(2):
                    mm = act.copy(h[:, 12 * k + 2 * n:12 * k + 2 * n + 2, :],
                                  bank(2 * n + k, 0, 384).rearrange("p (b e) -> p b e", b=2))
            mm.then_inc(s["image"], 1)
            act.wait_ge(s["b_r"], 1)
            act.copy(w1p[:, 1, :], w1f)
            act.copy(b1p[:, 1, :], b1f).then_inc(s["b_mid"], 1)
            act.wait_ge(s["ln_var"], 1)
            act.activation(lns[:, 3, :], lns[:, 2, :], ACT.Sqrt).then_inc(s["ln_std"], 1)

            def xn_out(n):
                act.wait_ge(s["xn_t"], LENT + n + 1)
                act.copy(xnT[:, :, 0, :], bank(4, 0, 2 * P).rearrange("p (x n) -> p x n", x=2))
                act.copy(xnT[0:D2, :, 1, :], bank(4, 2 * P, 4 * P, 0, D2)
                         .rearrange("p (x n) -> p x n", x=2)).then_inc(s["xn_e"], 1)

            xn_out(0)
            act.activation(act_carrier[:, :], ident[:, 0:1], ACT.Silu)
            act.wait_ge(s["st_w1"], 96)
            with act.Fori(0, 2) as bb:
                with act.Fori(0, CH) as c:
                    k = bb * CH + c
                    for x in range(2):
                        act.wait_ge(s["g0" if x == 0 else "g1s"], k + 1)
                        act.activation(gate[:, ds(k * 2 + x, 1), :, :].rearrange("p o g n -> p (o g n)"),
                                       bank(5 + 2 * x, 0, 384), ACT.Silu).then_inc(s[f"ge{x}"], 1)
                    xn_out(k + 1)
                    for x, kind in ((0, 1), (1, 0), (0, 0), (1, 1)):
                        what = "qk"[kind]
                        act.wait_ge(s[f"t{what}{x}"], k + 1)
                        act.wait_ge(s[f"o{x}"], LENT + k)
                        to = (0 if x else 4) + 2 * kind
                        act.copy(qkT[:, 2 * x + kind, :, :].rearrange("p h n -> p (h n)"),
                                 ps[:, to * 512:to * 512 + QK]).then_inc(s[f"e{what}{x}"], 1)
            act.wait_ge(s["gn_std"], 1)
            act.activation(gtmp[:, 3, :, :], gtmp[:, 2, :, :], ACT.Sqrt).then_inc(s["gn_std"], 1)
            act.wait_ge(s["ld_late"], 16 * 11)
            act.copy(sel[:, :, :].rearrange("p q n -> p (q n)"), x2T[0:96, :, :].rearrange("p a n -> p (a n)")).then_inc(s["sel_cast"], 1)
            act.wait_ge(s["gn_done"], 1)
            with act.Fori(0, 2) as bb:
                with act.Fori(0, CH // 2) as cb:
                    k = bb * (CH // 2) + cb
                    for x in range(4):
                        act.wait_ge(s["wo_s"], LENT + k * 4)
                        for g in range(VP):
                            col = (bb * 2 + x % 2) * VP + g
                            mm = act.activation(yg[:, x, g, :],
                                                oT[:, ds(k * 4 + x, 1), g, :].rearrange("p o n -> p (o n)"),
                                                ACT.Identity,
                                                bias=gbias[:, :, :].rearrange("p b g -> p (b g)")[:, ds(col, 1)],
                                                scale=gscale[:, :, :].rearrange("p b g -> p (b g)")[:, ds(col, 1)])
                        mm.then_inc(s["yn"], 1)
            act.wait_ge(s["ln_var"], 2)
            act.activation(lns[:, 3, :], lns[:, 2, :], ACT.Sqrt).then_inc(s["ln_std"], 1)
            act.wait_ge(s["sel_cast"], 1)

            def x2_out(i):
                act.wait_ge(s["x2_t"], LENT + i + 1)
                act.wait_ge(s["z_s"], LENT + i)
                act.copy(x2T[:, 0, :], bank(4))
                act.copy(x2T[0:D2, 1, :], bank(5, 0, 512, 0, D2)).then_inc(s["x2_e"], 1)

            def z_out(i):
                act.wait_ge(s["z_s"], LENT + i + 1)
                act.wait_ge(s["st_z"], LENT + 16 * i)
                act.copy(zT[:, ds(i * BLK, BLK)], bank(6))
                act.copy(zp[:, 0, :], bank(6)).then_inc(s["z_hi"], 1)

            def z_mid(i):
                act.wait_ge(s["z_r"], LENT + i + 1)
                act.copy(zp[:, 1, :], zr[:, :]).then_inc(s["z_mid"], 1)

            def copy_scores(tile):
                act.wait_ge(s["s_full"], LENT + tile + 1)
                act.wait_ge(s["p_taken"], LENT + tile)
                act.wait_ge(s["p_dist"], LENT + tile)
                act.copy(sc[:, :, 0:M], bank(7).rearrange("p (s m) -> p s m", m=M)).then_inc(s["s_copied"], 1)

            def exps(tile):
                act.wait_ge(s["p_dist"], LENT + tile + 1)
                act.activation(dist[:, :], dist[:, :], ACT.Exp).then_inc(s["e_done"], 1)

            def high_part(tile):
                act.wait_ge(s["t_full"], LENT + tile + 1)
                act.wait_ge(s["w_stored"], LENT + 48 * tile)
                act.copy(wp[:, 0, :, :].rearrange("p g n -> p (g n)"), bank(7)).then_inc(s["hi_done"], 1)
                act.wait_ge(s["b2_full"], LENT + tile)
                act.copy(wT[:, :, :].rearrange("p g n -> p (g n)"), bank(7)).then_inc(s["wT_done"], 1)

            x2_out(0)
            z_out(0)
            z_mid(0)
            act.wait_ge(s["ready"], 1)
            act.activation(act_carrier[:, :], ident[:, 0:1], ACT.Exp)
            with act.Fori(0, LEAD) as i:
                copy_scores(i)
                x2_out(i + 1)
                z_out(i + 1)
                exps(i)
                z_mid(i + 1)
                high_part(i)

            def iteration(i, prep):
                for n in range(8):
                    for j in range(4):
                        u = 4 * n + j
                        act.wait_ge(s["a_full"], UNITS * i + u + 1)
                        act.activation(ring[:, u % RING, :], bank(ABANK + u % TURNS), ACT.Gelu_apprx_tanh).then_inc(s["a_free"], 1)
                        if prep and u == 9:
                            copy_scores(i + LEAD)
                        if prep and u == 19:
                            exps(i + LEAD)
                        if prep and u == 29:
                            high_part(i + LEAD)

            act.wait_ge(s["cleared"], 1)
            act.activation(act_carrier[:, :], ident[:, 0:1], ACT.Gelu_apprx_tanh).then_inc(s["a_free"], TURNS)
            with act.Fori(0, NIT - LEAD) as i:
                iteration(i, True)
            with act.Fori(NIT - LEAD, NIT) as i:
                iteration(i, False)
            with act.Fori(0, NBLK) as i:
                act.wait_ge(s["fin_u"], i + 1)
                act.wait_ge(s["fin_o"], LENT + i)
                act.activation(uT[0:GH, :], bank(0, 0, 512, 0, GH), ACT.Gelu_apprx_tanh,
                               bias=g1b[:, :]).then_inc(s["fin_g"], 1)

        @block.vector
        def _(dve):
            links = [0]

            def link(ins):
                links[0] += 1
                ins.then_inc(s["dchain"], 1)
                dve.wait_ge(s["dchain"], links[0])

            dve.memset(h[:, TILES:TILES + 2, :], 0.0)
            dve.memset(stats[:, TILES:TILES + 2, :], 0.0)
            link(dve.memset(pix[:, :, :], 1.0))
            dve.wait_ge(s["ld_img"], 16 * 7)
            dve.tensor_scalar(row_hot[:, :], curve_bc[:, :, 1], iota_p[0:IMG, 0:1], None, ALU.is_equal).then_inc(s["hot"], 1)
            link(dve.tensor_copy(curve_f[:, :, :], curve_n[:, :, :]))
            for n in range(2):
                ins = dve.tensor_scalar(col_hot[:, n, :], iota_x[:, :], curve_f[:, n, 0:1], None, ALU.is_equal)
            link(ins)
            dve.wait_ge(s["b_hi"], 1)
            dve.tensor_tensor(w1f, w1f, w1p[:, 0, :], ALU.subtract)
            dve.tensor_tensor(b1f, b1f, b1p[:, 0, :], ALU.subtract).then_inc(s["b_r"], 1)
            dve.wait_ge(s["seen"], 1)
            for n in range(2):
                link(dve.tensor_tensor(picked.rearrange("p (k b x) -> p k b x", k=3, x=IMG),
                                       ps[:, 3 * n * 512:(3 * n + 3) * 512].rearrange("p (k f) -> p k f", k=3)[:, :, 0:384]
                                       .rearrange("p k (b x) -> p k b x", x=IMG),
                                       _mid2(col_hot[:, n, :], 3, 4), ALU.mult))
                ins = dve.tensor_reduce(pix[:, n, 0:B * CIN], picked.rearrange("p (n x) -> p n x", x=IMG), AXX, ALU.add)
                if n == 0:
                    link(ins)
            ins.then_inc(s["picked_s"], 1)

            def moments(n, extra):
                st = stats[:, :, :]
                link(dve.tensor_tensor(lns[:, 0, :], st[:, :, 1], st[:, :, 4], ALU.add))
                link(dve.tensor_scalar(mean[:, :], lns[:, 0, :], 0.5, None, ALU.mult))
                link(dve.tensor_tensor(lns[:, 1, :], st[:, :, 1], st[:, :, 4], ALU.subtract))
                link(dve.tensor_tensor(lns[:, 0, :], lns[:, 1, :], lns[:, 1, :], ALU.mult))
                link(dve.tensor_tensor(lns[:, 1, :], st[:, :, 2], st[:, :, 5], ALU.add))
                link(dve.tensor_scalar(lns[:, 1, :], lns[:, 1, :], 1.0 / D, EPS, ALU.mult, ALU.add))
                dve.scalar_tensor_tensor(lns[:, 2, :], lns[:, 0, :], 0.25, lns[:, 1, :], ALU.mult,
                                         ALU.add).then_inc(s["ln_var"], 1)
                dve.wait_ge(s["ln_std"], n)
                link(dve.reciprocal(rstd[:, :], lns[:, 3, :]))

            dve.wait_ge(s["b_mid"], 1)
            dve.wait_ge(s["b_r"], 1)
            dve.tensor_tensor(w1p[:, 2, :], w1f, w1p[:, 1, :], ALU.subtract)
            dve.tensor_tensor(b1p[:, 2, :], b1f, b1p[:, 1, :], ALU.subtract).then_inc(s["w1_lo"], 1)
            dve.wait_ge(s["image"], 1)
            dve.wait_ge(s["ld_text"], 64)
            with dve.Fori(0, TILES) as i:
                dve.bn_stats(stats[:, ds(i, 1), :].rearrange("p o k -> p (o k)"),
                             h[:, ds(i, 1), :].rearrange("p o e -> p (o e)")).then_inc(s["st1"], 1)
            dve.wait_ge(s["st1"], TILES)
            moments(1, 0)

            def xn_make(n):
                dve.wait_ge(s["xn_t"], LENT + n)
                for x in range(2):
                    ins = dve.tensor_scalar(xn[:, x, :], h[:, ds(n * 2 + x, 1), :].rearrange("p o e -> p (o e)"),
                                            mean[:, ds(n * 2 + x, 1)], rstd[:, ds(n * 2 + x, 1)],
                                            ALU.subtract, ALU.mult)
                ins.then_inc(s["xn_d"], 1)

            xn_make(0)
            dve.wait_ge(s["ld_attn"], 16 * 7)

            def table(c, n, a, b):
                v = rope[:, ds(c, 1), n, a:b].rearrange("p o d -> p (o d)")
                return _mid(v, H)

            def rotate(x, kind, k, c):
                what = "qk"[kind]
                to = 2 * kind
                src = ps[:, to * 512:to * 512 + QK].rearrange("p (h d) -> p h d", d=DQK)
                dve.wait_ge(s[f"{what}{x}"], k + 1)
                dve.wait_ge(s[f"a{what}{x}"], LENT + k)
                dve.wait_ge(s[f"o{x}"], LENT + k)
                n = 2 * x + kind
                hd = DQK // 2
                dve.tensor_tensor(t1[:, n, :, :], src, table(c, 2 * kind, 0, DQK), ALU.mult)
                dve.tensor_tensor(t2[:, n, :, 0:hd], src[:, :, hd:], table(c, 2 * kind + 1, 0, hd), ALU.mult)
                dve.tensor_tensor(t2[:, n, :, hd:], src[:, :, 0:hd], table(c, 2 * kind + 1, hd, DQK),
                                  ALU.mult).then_inc(s[f"r{what}{x}"], 1)

            def values(x, k, c):
                dve.wait_ge(s[f"v{x}"], k + 1)
                dve.tensor_tensor(vn[:, x, :, :], bank(4 + 2 * x, 0, HV).rearrange("p (h v) -> p h v", v=DV),
                                  _last(vscale[:, ds(c, 1), :].rearrange("p o h -> p (o h)"), DV),
                                  ALU.mult).then_inc(s[f"ve{x}"], 1)

            dve.wait_ge(s["w1_lo"], 1)
            dve.wait_ge(s["st_w1"], 96)
            with dve.Fori(0, 2) as bb:
                dve.wait_ge(s["o0"], LENT + bb * CH)
                dve.wait_ge(s["o1"], LENT + bb * CH)
                dve.wait_ge(s["se1"], LENT + bb * CH)
                dve.memset(state[:, :, :, :], 0.0).then_inc(s["reset"], 1)
                with dve.Fori(0, CH) as c:
                    k = bb * CH + c
                    rotate(0, 0, k, c)
                    rotate(0, 1, k, c)
                    values(0, k, c)
                    rotate(1, 0, k, c)
                    rotate(1, 1, k, c)
                    values(1, k, c)
                    xn_make(k + 1)
                    for x in range(2):
                        dve.wait_ge(s[f"sc{x}"], k + 1)
                        to = 4 + 2 * x
                        dve.tensor_tensor(pT[:, x, :, :], ps[:, to * 512:to * 512 + QK].rearrange("p (h n) -> p h n", n=P),
                                          _mid(causal[:, :], H), ALU.mult).then_inc(s[f"m{x}"], 1)
                    dve.wait_ge(s["reset"], bb + 1)
                    for x in range(2):
                        dve.wait_ge(s[f"o{x}"], LENT + k + 1)
                        dve.tensor_tensor(oT[:, ds(k * 2 + x, 1), :, :].rearrange("p o g n -> p (o g n)"),
                                          bank(2 * x, 0, HV),
                                          oscale[:, ds(c, 1), :, :].rearrange("p o g n -> p (o g n)"),
                                          ALU.mult).then_inc(s[f"oe{x}"], 1)
                        dve.wait_ge(s[f"se{x}"], LENT + k)
                        sx = state[:, x, :, :].rearrange("p h v -> p (h v)")
                        dve.tensor_tensor(sx, bank(2 * x + 1, 0, HV), sx, ALU.add).then_inc(s[f"se{x}"], 1)
                    for x in range(2):
                        dve.wait_ge(s[f"oe{x}"], LENT + k + 1)
                        for g in range(VP):
                            ins = dve.bn_stats(gns[:, ds(k * 2 + x, 1), g, :].rearrange("p o k -> p (o k)"),
                                               oT[:, ds(k * 2 + x, 1), g, :].rearrange("p o n -> p (o n)"))
                    ins.then_inc(s["st1"], 1)
            dve.wait_ge(s["st1"], TILES + PAIRS)
            attention_over(dve)
            for b in range(B):
                first = 12 * (b // 2) + b % 2
                for g in range(VP):
                    ins = dve.bn_aggr(gmv[:, b, g, :], gns[:, first:first + 11:2, g, :])
            ins.then_inc(s["gn_in"], 1)
            dve.wait_ge(s["gn_m"], 1)
            m1 = bank(0, 0, 24).rearrange("p (b g k) -> p b g k", b=B, g=VP)
            link(dve.tensor_tensor(gtmp[:, 0, :, :], gmv[:, :, :, 0], m1[:, :, :, 0], ALU.subtract))
            dve.tensor_tensor(gtmp[:, 1, :, :], gtmp[:, 0, :, :], gtmp[:, 0, :, :], ALU.mult).then_inc(s["gn_dev"], 1)
            link(dve.tensor_scalar(gtmp[:, 4, :, :], m1[:, :, :, 1], EPS, None, ALU.add))
            link(dve.tensor_copy(gtmp[:, 5, :, :], m1[:, :, :, 0]))
            dve.wait_ge(s["gn_v"], 1)
            dve.tensor_tensor(gtmp[:, 2, :, :], bank(1, 0, 12).rearrange("p (b g) -> p b g", b=B), gtmp[:, 4, :, :],
                              ALU.add).then_inc(s["gn_std"], 1)
            dve.wait_ge(s["gn_std"], 2)
            dve.wait_ge(s["ld_late"], 16 * 11)
            link(dve.reciprocal(gtmp[:, 0, :, :], gtmp[:, 3, :, :]))
            link(dve.tensor_tensor(gscale[:, :, :], gtmp[:, 0, :, :], _mid(gnw[:, :], B), ALU.mult))
            link(dve.tensor_tensor(gtmp[:, 4, :, :], gtmp[:, 5, :, :], gscale[:, :, :], ALU.mult))
            dve.tensor_tensor(gbias[:, :, :], _mid(gnb[:, :], B), gtmp[:, 4, :, :], ALU.subtract).then_inc(s["gn_done"], 1)
            with dve.Fori(0, NBLK) as k:
                for x in range(4):
                    dve.wait_ge(s["yn"], k * 4 + x + 1)
                    v = yg[:, x, :, :].rearrange("p g n -> p (g n)")
                    dve.tensor_tensor(v, v, gate[:, ds(k * 4 + x, 1), :, :].rearrange("p o g n -> p (o g n)"),
                                      ALU.mult).then_inc(s["yg_d"], 1)
                for x in range(4):
                    dve.wait_ge(s["wo_s"], LENT + k * 4 + x + 1)
                    hx = h[:, ds(k * 4 + x, 1), :].rearrange("p o e -> p (o e)")
                    dve.tensor_tensor(hx, bank(2 + x, 0, D), hx, ALU.add).then_inc(s["res"], 1)
                dve.wait_ge(s["res"], LENT + k * 4 + 4)
                for x in range(4):
                    ins = dve.bn_stats(stats[:, ds(k * 4 + x, 1), :].rearrange("p o k -> p (o k)"),
                                       h[:, ds(k * 4 + x, 1), :].rearrange("p o e -> p (o e)"))
                ins.then_inc(s["st1"], 1)
            dve.wait_ge(s["st1"], TILES + PAIRS + NBLK)
            dve.wait_ge(s["dchain"], links[0])
            moments(2, 0)
            dve.wait_ge(s["yg_d"], TILES)
            dve.memset(ysum[:, 0, :], 0.0)
            dve.memset(w2cur[:, 7, :, :], 0.0)
            dve.memset(uT[:, :], 1.0)
            dve.memset(sc[:, :, M:M + 4], FILLER)

            def x2_make(i):
                dve.wait_ge(s["x2_t"], LENT + i)
                for n in range(4):
                    ins = dve.tensor_scalar(x2[:, n, :], h[:, ds(i * 4 + n, 1), :].rearrange("p o e -> p (o e)"),
                                            mean[:, ds(i * 4 + n, 1)], rstd[:, ds(i * 4 + n, 1)],
                                            ALU.subtract, ALU.mult)
                ins.then_inc(s["x2_d"], 1)

            def z_rest(i):
                dve.wait_ge(s["z_hi"], i + 1)
                dve.wait_ge(s["z_lo"], LENT + i)
                dve.tensor_tensor(zr[:, :], bank(6), zp[:, 0, :], ALU.subtract).then_inc(s["z_r"], 1)

            def z_low(i):
                dve.wait_ge(s["z_mid"], i + 1)
                dve.wait_ge(s["z_r"], LENT + i + 1)
                dve.tensor_tensor(zp[:, 2, :], zr[:, :], zp[:, 1, :], ALU.subtract).then_inc(s["z_lo"], 1)

            def begin_sums(tile, blk, col):
                dve.wait_ge(s["b2_full"], LENT + tile + 1)
                dve.tensor_copy(ysum[:, ds(blk * 2 + 1, 2), ds(col, P)],
                         bank(7, 0, 2 * P).rearrange("p (a n) -> p a n", a=2)).then_inc(s["y_begun"], 1)

            def place_z(tile):
                dve.wait_ge(s["s_full"], LENT + tile)
                dve.tensor_copy(zcur[:, :], zT[:, ds(tile * P, P)]).then_inc(s["zc"], 1)

            def carry_waits():
                dve.memset(carrier[:, :], 0.0)

            def largest(tile, g0, g1):
                if g0 == 0:
                    dve.wait_ge(s["s_copied"], tile + 1)
                    dve.wait_ge(s["p_dist"], LENT + tile)
                    dve.wait_ge(s["p_taken"], LENT + tile)
                    carry_waits()
                for g in range(g0, g1):
                    ins = dve.max(top8[:, g, :], sc[:, g, 0:M])
                if g1 < S:
                    return
                ins.then_inc(s["t_top"], 1)
                dve.wait_ge(s["t_top"], tile * 3 + 1)
                dve.tensor_copy(top4[:, :, :], top8[:, :, 0:TOPK]).then_inc(s["t_top"], 1)
                dve.wait_ge(s["t_top"], tile * 3 + 2)
                dve.memset(top8[:, :, TOPK:8], FILLER).then_inc(s["t_top"], 1)

            def mark(tile, g0, g1):
                if g0 == 0:
                    dve.wait_ge(s["t_top"], tile * 3 + 3)
                    carry_waits()
                for g in range(g0, g1):
                    ins = dve.match_replace(mr[:, g, :], top8[:, g, :], sc[:, g, :], TAKEN)
                if g1 == S:
                    ins.then_inc(s["t_mr"], 1)

            def normaliser(tile):
                dve.wait_ge(s["e_done"], tile + 1)
                dve.wait_ge(s["p_w"], LENT + tile)
                dve.tensor_reduce(norm[:, 0, :], dist[:, S * M:].rearrange("p (s k) -> p s k", k=TOPK), AXX,
                                  ALU.add).then_inc(s["n_done"], 1)
                dve.wait_ge(s["n_done"], LENT + tile * 3 + 1)
                dve.tensor_scalar(norm[:, 0, :], norm[:, 0, :], -TAKEN, None, ALU.mult).then_inc(s["n_done"], 1)
                dve.wait_ge(s["n_done"], LENT + tile * 3 + 2)
                dve.reciprocal(norm[:, 1, :], norm[:, 0, :]).then_inc(s["n_done"], 1)

            x2_make(0)
            dve.memset(zst[96:99, :, :, :], 1.0).then_inc(s["ready"], 1)
            z_rest(0)
            z_low(0)
            dve.wait_ge(s["ready"], 1)
            with dve.Fori(0, LEAD) as i:
                place_z(i)
                x2_make(i + 1)
                largest(i, 0, S)
                mark(i, 0, S)
                z_rest(i + 1)
                normaliser(i)
                z_low(i + 1)
                begin_sums(i, i // 4, (i % 4) * P)
            dve.wait_ge(s["st_z"], LENT + 16 * NBLK)
            dve.memset(ring[:, RING - 4:RING, :], 0.0).then_inc(s["cleared"], 1)

            def keep_sums(i, slot, begun):
                dve.wait_ge(s["w2_done"], LENT + 8 * i + 1)
                dve.wait_ge(s["y_kept"], LENT + i)
                dve.wait_ge(s["y_begun"], LENT + begun)
                v = ysum[:, slot, :].rearrange("p o n -> p (o n)")
                dve.tensor_tensor(v, bank(6), v, ALU.add).then_inc(s["y_kept"], 1)

            def iteration(i, prep):
                for n in range(8):
                    for j in range(4):
                        u = 4 * n + j
                        dve.wait_ge(s["a_free"], UNITS * i + u + 1 + TURNS)
                        dve.wait_ge(s["w_full"], LENT + UNITS * i + u + 1)
                        dve.tensor_tensor(ring[:, u % RING, :], bank(WBANK + u % TURNS), ring[:, u % RING, :],
                                          ALU.mult).then_inc(s["w_free"], 1)
                        if prep and u == 0:
                            place_z(i + LEAD)
                        if prep and u in (9, 10):
                            largest(i + LEAD, 4 * (u - 9), 4 * (u - 8))
                        if prep and u in (12, 13):
                            mark(i + LEAD, 4 * (u - 12), 4 * (u - 11))
                        if prep and u == 17:
                            normaliser(i + LEAD)
                        if prep and u == 29:
                            begin_sums(i + LEAD, (i + LEAD) // 4, ((i + LEAD) % 4) * P)
                    if n == 0:
                        keep_sums(i, ds((i + 1) // 2, 1), i + LEAD - 1 if prep else TILES)

            dve.memset(carrier[:, :], 0.0).then_inc(s["w_free"], TURNS)
            with dve.Fori(0, NIT - LEAD) as i:
                iteration(i, True)
            with dve.Fori(NIT - LEAD, NIT) as i:
                iteration(i, False)
            keep_sums(NIT, slice(12, 13), TILES)
            dve.wait_ge(s["y_kept"], LENT + NIT + 1)
            dve.memset(carrier[:, :], 0.0).then_inc(s["fin_y"], NBLK)
            with dve.Fori(0, NBLK) as i:
                dve.wait_ge(s["fin_o"], LENT + i + 1)
                v = h[:, ds(i * 4, 4), :]
                src = ps[:, 512:5 * 512].rearrange("p (n f) -> p n f", n=4)[:, :, 0:D]
                dve.tensor_tensor(v, src, v, ALU.add).then_inc(s["fin_h"], 1)

        @block.gpsimd
        def _(pool):
            for n in lent:
                pool.nop().then_inc(s[n], LENT)
            with pool.Fori(0, PAIRS) as k:
                for x in range(2):
                    for kind, what in enumerate("qk"):
                        n = 2 * x + kind
                        pool.wait_ge(s[f"r{what}{x}"], k + 1)
                        pool.tensor_tensor(t1[:, n, :, :].rearrange("p h d -> p (h d)"),
                                           t1[:, n, :, :].rearrange("p h d -> p (h d)"),
                                           t2[:, n, :, :].rearrange("p h d -> p (h d)"),
                                           ALU.add).then_inc(s[f"a{what}{x}"], 1)

            def gates(tile):
                pool.wait_ge(s["p_em"], LENT + tile)
                pool.wait_ge(s["n_done"], LENT + tile * 3)
                pool.wait_ge(s["t_top"], tile * 3 + 3)
                pool.wait_ge(s["s_copied"], tile + 1)
                pool.tensor_tensor(dist[:, 0:S * M].rearrange("p (s m) -> p s m", m=M), sc[:, :, 0:M],
                                   _last(top4[:, :, 0], M), ALU.subtract)
                pool.tensor_tensor(dist[:, S * M:].rearrange("p (s k) -> p s k", k=TOPK), top4[:, :, :],
                                   _last(top4[:, :, 0], TOPK), ALU.subtract).then_inc(s["p_dist"], 1)
                pool.wait_ge(s["t_mr"], LENT + tile + 1)
                pool.tensor_tensor(taken[:, :, :], sc[:, :, 0:M], mr[:, :, 0:M], ALU.subtract).then_inc(s["p_taken"], 1)
                pool.wait_ge(s["p_taken"], LENT + tile + 1)
                pool.wait_ge(s["e_done"], tile + 1)
                pool.wait_ge(s["t_full"], LENT + tile)
                pool.tensor_tensor(taken[:, :, :], dist[:, 0:S * M].rearrange("p (s m) -> p s m", m=M),
                                   taken[:, :, :], ALU.mult).then_inc(s["p_em"], 1)
                pool.wait_ge(s["p_em"], LENT + tile + 1)
                pool.wait_ge(s["n_done"], LENT + tile * 3 + 3)
                pool.tensor_tensor(wn[:, :, :], taken[:, :, :], _last(norm[:, 1, :], M), ALU.mult).then_inc(s["p_w"], 1)
                pool.wait_ge(s["wT_done"], tile + 1)
                pool.tensor_tensor(wr[:, :, :], wT[:, :, :], wp[:, 0, :, :], ALU.subtract).then_inc(s["r_done"], 1)
                settle(pool)
                pool.wait_ge(s["r_done"], tile + 1)
                pool.tensor_copy(wp[:, 1, :, :], wr[:, :, :]).then_inc(s["mid_done"], 1)
                pool.wait_ge(s["mid_done"], tile + 1)
                pool.tensor_tensor(wp[:, 2, :, :], wr[:, :, :], wp[:, 1, :, :], ALU.subtract).then_inc(s["lo_done"], 1)

            pool.wait_ge(s["ready"], 1)
            with pool.Fori(0, TILES) as i:
                gates(i)


def _mid(v, n):
    return v.rearrange("p (o d) -> p o d", o=1).to_broadcast([v.shape[0], n, v.shape[1]])


def _mid2(v, n, m):
    return v.rearrange("p (o q d) -> p o q d", o=1, q=1).to_broadcast([v.shape[0], n, m, v.shape[1]])


def _last(v, n):
    return v.rearrange("p (d o) -> p d o", o=1).to_broadcast([v.shape[0], v.shape[1], n])


def _bcast(v, n):
    return v.rearrange("(o n) c -> o n c", o=1).to_broadcast([n, v.shape[0], v.shape[1]])


def _gate_rows(w_parts, k, a, kt, blk):
    v = w_parts[k, :, ds(blk * BLK, BLK)].rearrange("(a j e m) n -> a e m j n", a=2, j=4, e=2)
    return v[ds(a, 1), ds(kt, 1)].rearrange("a e m j n -> (a e m) j n")


def constants():
    import numpy as np

    pos = np.arange(T, dtype=np.float64)
    half = DQK // 2
    inv = 1.0 / 10000.0 ** (np.arange(half) / half)
    angle = (pos[:, None] * inv[None, :].astype(np.float32)).astype(np.float32).astype(np.float64)
    zeta = (np.arange(half) + half) / DQK
    grow = zeta[None, :] ** (pos[:, None] / 512.0)
    tabs = []
    for decay in (grow, 1.0 / grow):
        c, sn = np.cos(angle) * decay, np.sin(angle) * decay
        tabs += [np.concatenate([c, c], 1), np.concatenate([-sn, sn], 1)]
    rope = np.stack(tabs, 1).reshape(CH, P, 4, P).transpose(1, 0, 2, 3)
    gamma = 1.0 - 2.0 ** (-(5.0 + np.arange(H)))
    row = (1 - gamma[:, None] ** (pos[None, :] + 1)) / (1 - gamma[:, None])
    osc = gamma[:, None] ** pos[None, :] / np.sqrt(row) * DQK ** -0.5
    osc = np.repeat(osc.reshape(VP, 2, 1, T), DV, 2).reshape(VP, P, CH, P).transpose(1, 2, 0, 3)
    vsc = (gamma[None, :] ** -pos[:, None]).reshape(CH, P, H).transpose(1, 0, 2)
    sel = np.zeros((3, 32, 8, 4, HID))
    for m in range(32):
        sel[:, m, m // 4, m % 4, :] = 1
    halves = np.kron(np.eye(2), np.ones((DV, DV))) / DV
    f = np.float32
    return {"rope": rope.astype(f), "oscale": osc.astype(f), "vscale": vsc.astype(f),
            "causal": np.triu(np.ones((P, P))).astype(f), "ident": np.eye(P, dtype=f),
            "sel": sel.reshape(96, 2, BLK).astype(f), "halves": halves.astype(f),
            "iota_p": np.arange(P, dtype=f)[:, None], "iota_x": np.tile(np.arange(IMG, dtype=f), (P, 1))}


def layouts(i):
    import numpy as np

    g = {k: np.asarray(v) for k, v in i.items()}
    f = np.float32
    wblk = np.zeros((B * CIN + 1, B * D), f)
    for b in range(B):
        wblk[CIN * b:CIN * b + CIN, D * b:D * b + D] = g["L0_tok_proj_w"].T
        wblk[B * CIN, D * b:D * b + D] = g["L0_tok_proj_b"]
    cblk = np.zeros((S, R, S, M), f)
    for k in range(S):
        cblk[k, :, k, :] = g["L0_ffn_C"][k].T
    w2 = np.zeros((2, 2, 4, HID, 8, 4, 32), f)
    w2[..., 0:R] = g["L0_ffn_W2"].reshape(2, 4, 2, 8, 4, HID, R).transpose(0, 2, 4, 5, 3, 1, 6)
    b2 = np.zeros((2, M, 4, 4, 32), f)
    for k in range(S):
        b2[k % 2, :, k // 2, k % 4, 0:R] = g["L0_ffn_b2"][k]
    g1 = np.zeros((4, 32, 2, GH), f)
    g1[:, 0:R] = g["L0_ffn_G1"].reshape(2, 4, R, GH).transpose(1, 2, 0, 3)
    return {
        "x": g["x"], "txt": g["txt"], "curve": g["L0_tok_curve"], "wblk": wblk,
        "wcat": np.concatenate([g["L0_attn_Wq"], g["L0_attn_Wk"], g["L0_attn_Wv"], g["L0_attn_Wg"]], 1),
        "wo": g["L0_attn_Wo"], "gnw": g["L0_attn_gn_weight"].reshape(VP, P).T,
        "gnb": g["L0_attn_gn_bias"].reshape(VP, P).T,
        "pw": g["L0_ffn_P"].transpose(1, 0, 2).reshape(D, S * R), "cblk": cblk.reshape(P, S * M),
        "w1": g["L0_ffn_W1"].transpose(0, 2, 1, 3).reshape(P, M * HID), "b1": g["L0_ffn_b1"].reshape(P, P),
        "w2": w2.reshape(4, P, 1024), "b2": b2.reshape(P, 4, P), "g1": g1.reshape(P, 2, GH),
        "g1b": g["L0_ffn_g1b"].reshape(GH, 1), "g2": np.concatenate([g["L0_ffn_G2"], g["L0_ffn_g2b"][None]], 0),
    }


def kernel(**inputs):
    import concourse.bacc as bacc
    import numpy as np
    from concourse.bass_utils import run_bass_kernel_spmd

    nc = bacc.Bacc("TRN2", target_bir_lowering=False, num_devices=1)
    arrays, aps = {}, {}
    for name, a in {**layouts(inputs), **constants()}.items():
        a = np.ascontiguousarray(a)
        arrays[f"in_{name}"] = a
        aps[name] = nc.dram_tensor(f"in_{name}", a.shape, mybir.dt.from_np(a.dtype), kind="ExternalInput").ap()
    aps["out"] = nc.dram_tensor("out_h", (B, T, D), F32, kind="ExternalOutput").ap()
    fused_layer(nc, aps)
    r = run_bass_kernel_spmd(nc, [arrays], core_ids=[0])
    return r.results[0]["out_h"]
```
